# Optimizing a Trainium2 kernel written in Bass

```python
import numpy as np
import jax
import jax.numpy as jnp

def _softmax(x, axis=-1):
    return jax.nn.softmax(x, axis=axis)
def _gelu(x):
    return jax.nn.gelu(x, approximate=True)
def _silu(x):
    return jax.nn.silu(x)
def _sigmoid(x):
    return jax.nn.sigmoid(x)
def _layernorm(x, axis=-1, eps=1e-5):
    m = jnp.mean(x, axis=axis, keepdims=True)
    v = jnp.var(x, axis=axis, keepdims=True)
    return (x - m) / jnp.sqrt(v + eps)
def _scatter_add(tgt, idx, src, axis=0):
    return tgt.at[idx].add(src)
def _segment_sum(src, seg, n):
    return jax.ops.segment_sum(src, seg, n)

kernel_name = 'mk_adj_resnorm_d2_adj_128_08a8eb'

def setup_inputs(seed: int = 0):
    np.random.seed(seed)
    _w = jnp.asarray
    def _rec_inputs():
        import jax
        import jax.numpy as jnp
        _gk = jax.random.key(seed)
        x = -0.000929 + 1 * jax.random.normal(jax.random.fold_in(_gk, 1), (2708, 128), jnp.float32)
        _w = (1.0 + jnp.arange(2708, dtype=jnp.float32)) ** -0.5
        _w = _w / _w.mean()
        _pij = jnp.clip(0.00590842 * _w[:, None] * _w[None, :], 0.0, 1.0)
        _a = jax.random.uniform(jax.random.fold_in(_gk, 2), (2708, 2708)) < _pij
        _af = _a.astype(jnp.float32)
        adj = _af
        return x, adj
    x, adj = _rec_inputs()
    def _L0_gnn_setup():
        import jax, jax.numpy as jnp
        import numpy as np
        N, D = (8192, 128)
        EDGE_PROB = 0.005
        COS_EPS = 1e-08
        key = jax.random.key(seed)
        kx, ka = jax.random.split(key)
        x = jax.random.normal(kx, (N, D), dtype=jnp.float32)
        adj = (jax.random.uniform(ka, (N, N)) < EDGE_PROB).astype(jnp.float32)
        return {'t': jnp.float32(0.0), 'x': x, 'adj': adj, 'alpha': jnp.float32(0.5), 'beta': jnp.float32(1.0)}
    _L0_gnn_all = _L0_gnn_setup()
    _L0_gnn_in = {k: v for k, v in _L0_gnn_all.items() if k in ('t', 'alpha', 'beta', )}
    del _L0_gnn_all

    def _L1_gnn_setup():
        import jax, jax.numpy as jnp
        import numpy as np
        N_NODE = 4096
        N_FEA_IN = 128
        N_FEA_OUT = 128
        key = jax.random.key(seed)
        k_x, k_a, k_w, k_att = jax.random.split(key, 4)
        stdv_w = 1.0 / np.sqrt(N_FEA_OUT)
        stdv_a = 1.0 / np.sqrt(2 * N_FEA_OUT)
        X = jax.random.normal(k_x, (N_NODE, N_FEA_IN), dtype=jnp.float32)
        A = jax.random.uniform(k_a, (N_NODE, N_NODE), dtype=jnp.float32)
        W = jax.random.uniform(k_w, (N_FEA_IN, N_FEA_OUT), minval=-stdv_w, maxval=stdv_w, dtype=jnp.float32)
        a = jax.random.uniform(k_att, (1, 2 * N_FEA_OUT), minval=-stdv_a, maxval=stdv_a, dtype=jnp.float32)
        return {'X': X, 'A': A, 'W': W, 'a': a}
    _L1_gnn_all = _L1_gnn_setup()
    _L1_gnn_in = {k: v for k, v in _L1_gnn_all.items() if k in ('W', 'a', )}
    del _L1_gnn_all

    return {
        "x": x,
        "adj": adj,
        "L0_gnn_t": _L0_gnn_in["t"],
        "L0_gnn_alpha": _L0_gnn_in["alpha"],
        "L0_gnn_beta": _L0_gnn_in["beta"],
        "L1_gnn_W": _L1_gnn_in["W"],
        "L1_gnn_a": _L1_gnn_in["a"],
    }

def reference(x, adj, L0_gnn_t, L0_gnn_alpha, L0_gnn_beta, L1_gnn_W, L1_gnn_a):
    import jax
    import jax.numpy as jnp
    def _L0_gnn_ref(t, x, adj, alpha, beta):
        import jax, jax.numpy as jnp
        import numpy as np
        N, D = (8192, 128)
        EDGE_PROB = 0.005
        COS_EPS = 1e-08
        deg = jnp.clip(adj.sum(axis=1), 1.0)
        dis = deg ** (-0.5)
        adj_norm = dis[:, None] * adj * dis[None, :]
        diffusion = adj_norm @ x - x
        norms = jnp.maximum(jnp.linalg.norm(x, axis=-1), COS_EPS)
        sim = x @ x.T / (norms[:, None] * norms[None, :])
        attn = jax.nn.softmax(beta * sim * adj, axis=1)
        attn = jax.lax.stop_gradient(attn)
        return diffusion + jax.nn.sigmoid(alpha) * (attn @ x - x)

    def _L1_gnn_ref(X, A, W, a):
        import jax, jax.numpy as jnp
        import numpy as np
        N_NODE = 4096
        N_FEA_IN = 128
        N_FEA_OUT = 128
        XW = jnp.matmul(X, W)
        f = W.shape[1]
        s_col = jnp.matmul(XW, a[0, :f])
        s_row = jnp.matmul(XW, a[0, f:])
        Z1 = jax.nn.leaky_relu(s_row[:, None] + s_col[None, :], negative_slope=0.01)
        den = jnp.exp(Z1)
        num = jnp.matmul(A, den)
        att = jnp.where(num != 0, den / jnp.where(num != 0, num, 1.0), 0.0)
        H = jnp.matmul(A, jnp.matmul(att, XW))
        return H

    x = _layernorm(x + _L0_gnn_ref(L0_gnn_t, x, adj, L0_gnn_alpha, L0_gnn_beta), axis=-1)
    x = _layernorm(x + _L1_gnn_ref(x, adj, L1_gnn_W, L1_gnn_a), axis=-1)
    return x


_drawn_inputs = setup_inputs


def setup_inputs(seed=0):
    import zlib

    import numpy as np

    out = dict(_drawn_inputs(seed))
    spreads = {}
    factors = {}
    for name, (base, spread) in spreads.items():
        noise = np.random.default_rng([zlib.crc32(name.encode()), seed]).standard_normal(out[name].shape)
        drawn = base * np.exp(spread * noise) if base else spread * noise
        out[name] = jnp.asarray(drawn.astype(out[name].dtype))
    for name, factor in factors.items():
        out[name] = (out[name] * factor).astype(out[name].dtype)
    return out
```

```python
from contextlib import ExitStack

import concourse.bass as bass
from concourse import mybir

P = 128
N = 2708
T = 22
NP = T * P
D = 128
LAST = N - (T - 1) * P
CH = [(c * 452, min(452, N - c * 452)) for c in range(6)]
SIMC = [(0, 1024), (1024, 1024), (2048, N - 2048)]
GRP = [(g * 4, min(4, T - g * 4)) for g in range(6)]
XS = 1024.0
SLOPE = 0.01
LN_EPS = 1e-5
COS_EPS = 1e-8

ALU = mybir.AluOpType
ACT = mybir.ActivationFunctionType
AX = mybir.AxisListType
F32 = mybir.dt.float32
BF16 = mybir.dt.bfloat16
FP16 = mybir.dt.float16


class Line:

    def __init__(self, sem):
        self.sem = sem
        self.n = 0
        self.items = []
        self.met = {}

    def wait(self, *marks):
        for mark in marks:
            if mark is None:
                continue
            sem, v = mark
            if self.met.get(id(sem), 0) < v:
                self.met[id(sem)] = v
                self.items.append(("wait", sem, v, None))

    def do(self, fn, *a, **k):
        self.items.append(("quiet", fn, a, k))

    def sig(self, fn, *a, **k):
        self.n += 1
        self.items.append(("sig", fn, a, k))
        return (self.sem, self.n)

    def dma(self, sem, fn, *a, **k):
        self.items.append(("dma", fn, a, (k, sem)))

    def emit(self, eng):
        for kind, x, a, k in self.items:
            if kind == "wait":
                eng.wait_ge(x, a)
            elif kind == "quiet":
                x(*a, **k)
            elif kind == "sig":
                x(*a, **k).then_inc(self.sem, 1)
            else:
                x(*a, **k[0]).then_inc(k[1], 16)


def adj_resnorm2_kernel(nc, x, adj, adjT, alpha, beta, W, a, out):
    with ExitStack() as ctx:
        def sb(name, shape, dt=F32):
            return ctx.enter_context(nc.sbuf_tensor(name, shape, dt))

        def sem(name):
            return ctx.enter_context(nc.semaphore(name))

        AT = sb("AT", [P, T, N], BF16)
        R1 = sb("R1", [P, 11264])
        X = sb("X", [P, NP])
        AO = sb("AO", [P, NP])
        XN = sb("XN", [P, NP])
        Wt = sb("Wt", [P, D])
        ident = sb("ident", [P, P])
        arep = sb("arep", [P, 2, P])
        ac = sb("ac", [P, 2])[:, :]
        sm = sb("sm", [P, 12])
        st = sb("st", [P, 10, T])
        mx = sb("mx", [P, 2, 4])
        ln = sb("ln", [P, 2, 12])
        hb = sb("hb", [P, 2, D])
        tA = sb("tA", [P, 2, 452])
        tB = sb("tB", [P, 2, 452])
        tC = sb("tC", [P, 452])

        PSALL = ctx.enter_context(nc.psum_tensor("PSALL", [P, 8, 512], F32))

        X3 = X[:, :].rearrange("p (t d) -> p t d", t=T)
        AO3 = AO[:, :].rearrange("p (t d) -> p t d", t=T)
        Ab = [R1[:, s * NP:(s + 1) * NP] for s in range(3)]
        junk = R1[:, 3 * NP:3 * NP + NP // 2].bitcast(BF16)
        ET = [R1[:, 3 * NP + NP // 2 + s * 512:3 * NP + NP // 2 + (s + 1) * 512].rearrange("p (b i) -> p b i", b=4)
              for s in range(2)]
        xnh = XN[:, 0:NP // 2].bitcast(FP16)
        xnl = XN[:, NP // 2:NP].bitcast(FP16)
        xp = R1[:, 0:3 * NP // 2].bitcast(BF16).rearrange("p (t c d) -> p t c d", t=T, c=3)
        XW = XN[:, :].rearrange("p (t d) -> p t d", t=T)
        cb = X[:, :]
        rb = R1[:, 3 * NP:4 * NP]
        x1T = R1[:, 2 * NP:3 * NP]
        XWT = R1[:, 1 * NP:2 * NP]
        dz = R1[:, 0:NP]
        dz3 = dz.rearrange("p (t j) -> p t j", t=T)
        dh = [R1[:, NP + s * NP:NP + s * NP + NP // 2].bitcast(BF16) for s in range(2)]
        dl = [R1[:, NP + s * NP + NP // 2:2 * NP + s * NP].bitcast(BF16) for s in range(2)]
        bcol, sig, eal, one = sm[:, 0:1], sm[:, 1:2], sm[:, 2:3], sm[:, 3:4]
        braw, araw = sm[:, 4:5], sm[:, 5:6]
        epsc = sm[:, 6:7]
        half, mhalf = sm[:, 7:8], sm[:, 8:9]
        sq, nrm, rn, deg, dis, rs, rrs, scol, srow, scol1 = (st[:, i, :] for i in range(10))

        s_pe, s_dv, s_ac, s_gp = sem("s_pe"), sem("s_dv"), sem("s_ac"), sem("s_gp")
        s_x, s_w, s_const = sem("s_x"), sem("s_w"), sem("s_const")
        s_A = [sem(f"s_A{i}") for i in range(3)]
        s_AT = sem("s_AT")
        s_out = [sem(f"s_out{i}") for i in range(2)]

        pe, dv, ac_, gp, sp = Line(s_pe), Line(s_dv), Line(s_ac), Line(s_gp), Line(None)
        V, S, G, TE = nc.vector, nc.scalar, nc.gpsimd, nc.tensor

        sp.dma(s_x, nc.sync.dma_start, X3, x.rearrange("(t p) d -> p t d", p=P))
        x_in = (s_x, 16)
        small = [(Wt[:, :], W), (ac, a),
                 (braw, beta.broadcast_to([P, 1])), (araw, alpha.broadcast_to([P, 1]))]
        A_in = {}
        A_free = {}

        def load_A(it):
            s = it % 3
            if it >= 3:
                sp.wait(A_free[it - 3])
            sp.dma(s_A[s], nc.sync.dma_start, Ab[s], adj[it * P:(it + 1) * P, :])
            A_in[it] = (s_A[s], 16 * (it // 3 + 1))

        load_A(0)
        for dst, src in small:
            sp.dma(s_w, nc.sync.dma_start, dst, src)
        w_in = (s_w, 16 * len(small))
        load_A(1)
        load_A(2)

        m = gp.sig(G.memset, ident[:, :], 0.0)
        gp.wait(m)
        id_ok = gp.sig(G.affine_select, out=ident[:, :], in_=ident[:, :], compare_op=ALU.not_equal, fill=1.0,
                       base=0, pattern=[[-1, P]], channel_multiplier=1)
        gp.sig(G.memset, half, 0.5)
        pc_ok = gp.sig(G.memset, mhalf, -0.5)
        for kt in range(T):
            gp.dma(s_AT, G.dma_start, AT[:, kt, :], adjT[kt * P:(kt + 1) * P, :])
        AT_in = (s_AT, 16 * T)

        xx = AO3
        dv.wait(x_in)
        m = dv.sig(V.tensor_tensor, xx, X3, X3, ALU.mult)
        dv.wait(m)
        m = dv.sig(V.tensor_reduce, sq, xx, AX.X, ALU.add)
        gp.wait(m, pc_ok)
        m = gp.sig(G.tensor_tensor, nrm, sq, half.broadcast_to([P, T]), ALU.pow)
        dv.wait(m)
        m = dv.sig(V.tensor_scalar, nrm, nrm, COS_EPS, 1.0 / XS, ALU.max, ALU.mult)
        dv.wait(m)
        m = dv.sig(V.reciprocal, rn, nrm)
        dv.wait(m)
        xn_ok = dv.sig(V.tensor_tensor, AO3, X3, rn.unsqueeze(2).broadcast_to([P, T, D]), ALU.mult)
        pe.wait(xn_ok, id_ok)
        free = [None, None]
        split = None
        for g, (t0, nb) in enumerate(GRP):
            b = g % 2
            pe.wait(free[b])
            for q in range(nb):
                m = pe.sig(TE.transpose, PSALL[:, b, q * P:(q + 1) * P], AO3[:, t0 + q, :], ident[:, :])
            w = nb * P
            c0 = t0 * P
            dv.wait(m)
            h = dv.sig(V.tensor_copy, xnh[:, c0:c0 + w], PSALL[:, b, 0:w])
            dv.wait(h)
            split = free[b] = dv.sig(V.tensor_tensor, xnl[:, c0:c0 + w], PSALL[:, b, 0:w], xnh[:, c0:c0 + w],
                                     ALU.subtract)
        ao_free = m
        ac_.wait(w_in)
        e = ac_.sig(S.activation, eal, araw, ACT.Exp, scale=-1.0)
        dv.wait(e)
        m = dv.sig(V.tensor_scalar, eal, eal, 1.0, None, ALU.add)
        dv.wait(m)
        sig_ok = dv.sig(V.reciprocal, sig, eal)
        dv.wait(w_in)
        ar_ok = dv.sig(V.tensor_copy, arep[:, :, :], ac.unsqueeze(2).broadcast_to([P, 2, P]))
        bc_ok = dv.sig(V.tensor_scalar, bcol, braw, 1.0 / (XS * XS), None, ALU.mult)

        ps_free = [split, split, split, split]
        pair = 0
        exp_done = {}
        sub_ao = {}

        def sim(it):
            nonlocal pair
            s = it % 3
            ac_.wait(A_in[it])
            d = ac_.sig(S.activation, junk, Ab[s], ACT.Copy, accum_out=deg[:, it:it + 1])
            if it >= 2:
                dv.wait(exp_done[it - 2])
            for c, (c0, w) in enumerate(SIMC):
                b = pair % 2
                pair += 1
                pe.wait(ps_free[b])
                for o in range(0, w, 512):
                    ww = min(512, w - o)
                    dst = PSALL[:, 2 * b + o // 512, 0:ww]
                    k = 0
                    for lh, rh in ((xnh, xnh), (xnh, xnl), (xnl, xnh)):
                        args = (dst, lh[:, it * P:(it + 1) * P], rh[:, c0 + o:c0 + o + ww])
                        kw = dict(start=(k == 0), stop=(k == 2))
                        if k == 2 and o + 512 >= w:
                            m = pe.sig(TE.matmul, *args, **kw)
                        else:
                            pe.do(TE.matmul, *args, **kw)
                        k += 1
                dv.wait(m, A_in[it], d, bc_ok)
                src = PSALL[:, 2 * b:2 * b + 2, :].rearrange("p b n -> p (b n)")[:, 0:w]
                ps_free[b] = l = dv.sig(V.tensor_tensor_reduce, out=Ab[s][:, c0:c0 + w], in0=src,
                                        in1=Ab[s][:, c0:c0 + w], scale=bcol, scalar=-3.4e38,
                                        op0=ALU.mult, op1=ALU.max, accum_out=mx[:, it % 2, c:c + 1])
            dv.wait(l)
            r = dv.sig(V.tensor_reduce, mx[:, it % 2, 3:4], mx[:, it % 2, 0:3], AX.X, ALU.max)
            dv.wait(r)
            r = dv.sig(V.tensor_scalar, mx[:, it % 2, 3:4], mx[:, it % 2, 3:4], -1.0, None, ALU.mult)
            ac_.wait(r)
            exp_done[it] = ac_.sig(S.activation, Ab[s][:, 0:N], Ab[s][:, 0:N], ACT.Exp, bias=mx[:, it % 2, 3:4],
                                   accum_out=rs[:, it:it + 1])

        pt_free = [split, split]
        et_free = [None, None]
        po_free = [None, None]
        tg = 0

        def attend(it):
            nonlocal tg
            s = it % 3
            pe.wait(exp_done[it])
            po = PSALL[:, 6 + it % 2, 0:D]
            pend = None

            def mm(t0, nb, e, ok):
                pe.wait(ok)
                if t0 == 0:
                    pe.wait(po_free[it % 2])
                for q in range(nb):
                    args = (po, ET[e][:, q, :], X3[:, t0 + q, :])
                    kw = dict(start=(t0 + q == 0), stop=(t0 + q == T - 1))
                    if q == nb - 1:
                        et_free[e] = pe.sig(TE.matmul, *args, **kw)
                    else:
                        pe.do(TE.matmul, *args, **kw)

            for t0, nb in GRP:
                b = tg % 2
                pe.wait(pt_free[b])
                for q in range(nb):
                    src = Ab[s][:, (t0 + q) * P:(t0 + q + 1) * P]
                    dst = PSALL[:, 4 + b, q * P:(q + 1) * P]
                    if q == nb - 1:
                        m = pe.sig(TE.transpose, dst, src, ident[:, :])
                    else:
                        pe.do(TE.transpose, dst, src, ident[:, :])
                if pend is not None:
                    mm(*pend)
                ev = dv if tg % 2 else ac_
                ev.wait(m, et_free[b])
                dstv = ET[b][:, 0:nb, :].rearrange("p b i -> p (b i)")
                srcv = PSALL[:, 4 + b, 0:nb * P]
                if tg % 2:
                    ok = dv.sig(V.tensor_copy, dstv, srcv)
                else:
                    ok = ac_.sig(S.activation, dstv, srcv, ACT.Copy)
                pt_free[b] = ok
                pend = (t0, nb, b, ok)
                tg += 1
            A_free[it] = m
            mm(*pend)
            att = et_free[pend[2]]
            dv.wait(exp_done[it])
            r = dv.sig(V.reciprocal, rrs[:, it:it + 1], rs[:, it:it + 1])
            dv.wait(r, att, ao_free)
            po_free[it % 2] = sub_ao[it] = dv.sig(V.scalar_tensor_tensor, AO3[:, it, :], po, rrs[:, it:it + 1],
                                                  X3[:, it, :], ALU.mult, ALU.subtract)

        sim(0)
        for it in range(T):
            if it + 1 < T:
                sim(it + 1)
            attend(it)
            if it + 3 < T:
                load_A(it + 3)

        def split3(src3, dst, tmp, first, slices):
            done = []
            for (t0, nt) in slices:
                sl = src3[:, t0:t0 + nt, :]
                dv.wait(*first)
                h = dv.sig(V.tensor_copy, dst[:, t0:t0 + nt, 0, :], sl)
                dv.wait(h)
                r = dv.sig(V.tensor_tensor, sl, sl, dst[:, t0:t0 + nt, 0, :], ALU.subtract)
                dv.wait(r)
                h = dv.sig(V.tensor_copy, dst[:, t0:t0 + nt, 1, :], sl)
                dv.wait(h)
                done.append(dv.sig(V.tensor_tensor, dst[:, t0:t0 + nt, 2, :], sl, dst[:, t0:t0 + nt, 1, :],
                                   ALU.subtract))
            return done

        SL = [(0, 6), (6, 6), (12, 6), (18, 4)]
        xd3 = R1[:, 3 * NP:4 * NP].rearrange("p (t d) -> p t d", t=T)
        att_end = et_free[(tg - 1) % 2]
        dv.wait(att_end)
        m = dv.sig(V.tensor_scalar, dis, deg, 1.0, None, ALU.max)
        gp.wait(m)
        m = gp.sig(G.tensor_tensor, dis, dis, mhalf.broadcast_to([P, T]), ALU.pow)
        dv.wait(m)
        m = dv.sig(V.tensor_tensor, xd3, X3, dis.unsqueeze(2).broadcast_to([P, T, D]), ALU.mult)
        xp_ok = split3(xd3, xp, None, (m,), SL)

        bank_free = [sub_ao[T - 1]] * 8
        sq_dve = sub_ao[T - 1]
        hb_free = [None, None]
        x1_ok = {}

        def spread(it, parts_ok, bank):
            mrow = P if it < T - 1 else LAST
            pe.wait(bank_free[bank])
            for jt in range(T):
                for (t0, nt), ok in zip(SL, parts_ok):
                    if jt == t0:
                        pe.wait(ok)
                args = (PSALL[0:mrow, bank, 0:3 * D], AT[:, jt, it * P:it * P + mrow],
                        xp[:, jt, :, :].rearrange("p c d -> p (c d)"))
                kw = dict(start=(jt == 0), stop=(jt == T - 1))
                if jt == T - 1:
                    m = pe.sig(TE.matmul, *args, **kw)
                else:
                    pe.do(TE.matmul, *args, **kw)
            return m, mrow, PSALL[0:mrow, bank, 0:3 * D].rearrange("p (c d) -> p d c", c=3)

        def norm(h, mrow, it, dst, ok):
            s = it % 2
            dv.wait(ok)
            b = dv.sig(V.bn_stats, ln[0:mrow, s, 0:6], h)
            dv.wait(b)
            b = dv.sig(V.bn_aggr, ln[0:mrow, s, 6:8], ln[0:mrow, s, 0:6])
            dv.wait(b)
            b = dv.sig(V.tensor_scalar, ln[0:mrow, s, 8:9], ln[0:mrow, s, 7:8], LN_EPS, None, ALU.add)
            gp.wait(b)
            b = gp.sig(G.tensor_tensor, ln[0:mrow, s, 9:10], ln[0:mrow, s, 8:9], mhalf[0:mrow, :], ALU.pow)
            return b, (lambda: (dv.wait(b), dv.sig(V.tensor_scalar, dst, h, ln[0:mrow, s, 6:7],
                                                   ln[0:mrow, s, 9:10], ALU.subtract, ALU.mult))[1])

        pe.wait(AT_in)
        late = None
        gz = gp.sig(G.memset, hb[:, :, :], 0.0)

        def layer0_tail(it, m, mrow, view):
            s = it % 2
            hh = hb[0:mrow, s, :]
            dv.wait(m, hb_free[s], sig_ok, gz)
            r = dv.sig(V.tensor_reduce, hh, view, AX.X, ALU.add)
            bank_free[it % 4] = r
            dv.wait(r)
            r = dv.sig(V.scalar_tensor_tensor, hh, hh, dis[0:mrow, it:it + 1], X3[0:mrow, it, :],
                       ALU.mult, ALU.subtract)
            dv.wait(r)
            r = dv.sig(V.scalar_tensor_tensor, hh, AO3[0:mrow, it, :], sig[0:mrow, :], hh, ALU.mult, ALU.add)
            dv.wait(r)
            r = dv.sig(V.tensor_tensor, hh, hh, X3[0:mrow, it, :], ALU.add)
            return norm(hh, mrow, it, AO3[0:mrow, it, :], r)

        def flush(item):
            it, fin = item
            if it == T - 1:
                z = dv.sig(V.memset, AO3[:, it, :], 0.0)
                dv.wait(z)
            x1_ok[it] = hb_free[it % 2] = fin()

        for it in range(T):
            m, mrow, view = spread(it, xp_ok, it % 4)
            if it == T - 1:
                flush(late)
                late = None
            _, fin = layer0_tail(it, m, mrow, view)
            if late is not None:
                flush(late)
            late = (it, fin)
        flush(late)

        p2_end = m
        groups = []
        bfree = dict((b, x1_ok[T - 1]) for b in range(8))
        x1T_ok = []
        dv.wait(p2_end)
        for g, (t0, nb) in enumerate(GRP):
            b = g % 2
            pe.wait(x1_ok[t0 + nb - 1], bfree[b])
            for q in range(nb):
                m = pe.sig(TE.transpose, PSALL[:, b, q * P:(q + 1) * P], AO3[:, t0 + q, :], ident[:, :])
            dv.wait(m)
            ok = bfree[b] = dv.sig(V.tensor_copy, x1T[:, t0 * P:(t0 + nb) * P], PSALL[:, b, 0:nb * P])
            x1T_ok.append(ok)
        for g, (t0, nb) in enumerate(GRP):
            c0, w = t0 * P, nb * P
            b = 2 + g % 2
            pe.wait(x1T_ok[g], bfree[b])
            m = pe.sig(TE.matmul, PSALL[:, b, 0:w], Wt[:, :], x1T[:, c0:c0 + w], start=True, stop=True)
            ac_.wait(m)
            xwt_ok = bfree[b] = ac_.sig(S.activation, XWT[:, c0:c0 + w], PSALL[:, b, 0:w], ACT.Copy)
            b = 4 + g % 2
            pe.wait(bfree[b])
            for q in range(nb):
                m = pe.sig(TE.matmul, PSALL[:, b, q * P:(q + 1) * P], x1T[:, c0 + q * P:c0 + (q + 1) * P], Wt[:, :],
                           start=True, stop=True)
            dv.wait(m)
            xw_ok = bfree[b] = dv.sig(V.tensor_copy, XW[:, t0:t0 + nb, :],
                                      PSALL[:, b, 0:w].rearrange("p (b d) -> p b d", b=nb))
            groups.append((c0, w, xwt_ok))
        for g, (c0, w, ok) in enumerate(groups):
            pe.wait(ok, ar_ok)
            b = g % 2
            pe.wait(bfree[b])
            m = pe.sig(TE.matmul, PSALL[:, b, 0:w], arep[:, 0, :], XWT[:, c0:c0 + w], start=True, stop=True)
            dv.wait(m)
            bfree[b] = cb_ok = dv.sig(V.tensor_copy, cb[:, c0:c0 + w], PSALL[:, b, 0:w])
            b = 2 + g % 2
            pe.wait(bfree[b])
            m = pe.sig(TE.matmul, PSALL[:, b, 0:w], arep[:, 1, :], XWT[:, c0:c0 + w], start=True, stop=True)
            ac_.wait(m)
            bfree[b] = rb_ok = ac_.sig(S.activation, rb[:, c0:c0 + w], PSALL[:, b, 0:w], ACT.Copy)
        pe.wait(bfree[4], bfree[5])
        for t in range(T):
            m = pe.sig(TE.matmul, PSALL[:, 4, 2 * t:2 * t + 2], XWT[:, t * P:(t + 1) * P], arep[:, :, 0],
                       start=True, stop=True)
        dv.wait(m)
        sc = PSALL[:, 4, 0:2 * T].rearrange("p (t c) -> p c t", c=2)
        c_ok = dv.sig(V.tensor_copy, scol, sc[:, 0, :])
        r_ok = dv.sig(V.tensor_copy, srow, sc[:, 1, :])
        xwt_free = m
        dv.wait(c_ok)
        c_ok = dv.sig(V.tensor_scalar, scol1, scol, SLOPE, None, ALU.mult)

        num_free = {6: r_ok, 7: r_ok}
        y_free = [r_ok, cb_ok, rb_ok, xw_ok]
        den_ok = {}
        den_free = {}
        dz_free = None

        def den(jt):
            nonlocal dz_free
            s = jt % 2
            gp.wait(cb_ok, r_ok, xwt_free, dz_free)
            z = gp.sig(G.tensor_tensor, dz3, cb[:, jt * P:(jt + 1) * P].unsqueeze(1).broadcast_to([P, T, P]),
                       srow.unsqueeze(2).broadcast_to([P, T, P]), ALU.add)
            dv.wait(z)
            z = dv.sig(V.scalar_tensor_tensor, dz, dz, SLOPE, dz, ALU.mult, ALU.max)
            ac_.wait(z)
            z = ac_.sig(S.activation, dz, dz, ACT.Exp)
            ac_.wait(z, den_free.get(jt - 2))
            h = ac_.sig(S.activation, dh[s], dz, ACT.Copy)
            dv.wait(z, h)
            dz_free = den_ok[jt] = dv.sig(V.tensor_tensor, dl[s], dz, dh[s], ALU.subtract)

        tb_free = [None, None]
        tc_free = None
        ta_free = [None, None]
        den(0)
        pending = None
        u = 0
        y_end = None

        def ymm(jt, c, g_ok, s):
            c0, w = CH[c]
            pe.wait(g_ok)
            if jt == 0:
                pe.wait(*y_free)
            return pe.sig(TE.matmul, PSALL[:, c, 0:w], XW[:, jt, :], tB[:, s, 0:w], start=(jt == 0), stop=(jt == T - 1))

        for jt in range(T):
            ds = jt % 2
            for c, (c0, w) in enumerate(CH):
                s = u % 2
                b = 6 + s
                ac_.wait(rb_ok, c_ok, ta_free[s])
                e1 = ac_.sig(S.activation, tA[:, s, 0:w], rb[:, c0:c0 + w], ACT.Exp, bias=scol[:, jt:jt + 1])
                ac_.wait(tc_free)
                e2 = ac_.sig(S.activation, tC[:, 0:w], rb[:, c0:c0 + w], ACT.Exp, bias=scol1[:, jt:jt + 1],
                             scale=SLOPE)
                dv.wait(e1, e2)
                e_ok = tc_free = dv.sig(V.tensor_tensor, tA[:, s, 0:w], tA[:, s, 0:w], tC[:, 0:w], ALU.max)
                pe.wait(den_ok[jt], num_free[b])
                for kt in range(T):
                    for part, q in ((dh[ds], 0), (dl[ds], 1)):
                        args = (PSALL[:, b, 0:w], part[:, kt * P:(kt + 1) * P], AT[:, kt, c0:c0 + w])
                        kw = dict(start=(kt == 0 and q == 0), stop=(kt == T - 1 and q == 1))
                        if kt == T - 1 and q == 1:
                            m = pe.sig(TE.matmul, *args, **kw)
                        else:
                            pe.do(TE.matmul, *args, **kw)
                if pending is not None:
                    tb_free[pending[3]] = y_end = ymm(*pending)
                ac_.wait(m, tb_free[s])
                n0 = ac_.sig(S.activation, tB[:, s, 0:w], PSALL[:, b, 0:w], ACT.Copy)
                dv.wait(n0, e_ok)
                n1 = dv.sig(V.scalar_tensor_tensor, tB[:, s, 0:w], PSALL[:, b, 0:w], 0.0, tB[:, s, 0:w],
                            ALU.is_equal, ALU.add)
                n2 = dv.sig(V.scalar_tensor_tensor, tA[:, s, 0:w], PSALL[:, b, 0:w], 0.0, tA[:, s, 0:w],
                            ALU.not_equal, ALU.mult)
                dv.wait(n1)
                n3 = dv.sig(V.reciprocal, tB[:, s, 0:w], tB[:, s, 0:w])
                dv.wait(n3)
                g_ok = ta_free[s] = dv.sig(V.tensor_tensor, tB[:, s, 0:w], tB[:, s, 0:w], tA[:, s, 0:w], ALU.mult)
                num_free[b] = n2
                pending = (jt, c, g_ok, s)
                if c == 1 and jt + 1 < T:
                    den(jt + 1)
                u += 1
            den_free[jt] = m
        y_end = ymm(*pending)

        YT = R1[:, 3 * NP:4 * NP]
        Y3 = R1[:, 2 * NP:3 * NP].rearrange("p (t d) -> p t d", t=T)
        gp.wait(y_end, g_ok)
        yz = gp.sig(G.memset, YT[:, N:NP], 0.0)
        for c, (c0, w) in enumerate(CH):
            ev = ac_ if c % 2 else dv
            ev.wait(y_end, g_ok)
            if c % 2:
                yt_a = ac_.sig(S.activation, YT[:, c0:c0 + w], PSALL[:, c, 0:w], ACT.Copy)
            else:
                yt_d = dv.sig(V.tensor_copy, YT[:, c0:c0 + w], PSALL[:, c, 0:w])
        pe.wait(yt_a, yt_d, yz)
        bfree = {0: yt_a, 1: yt_a}
        for g, (t0, nb) in enumerate(GRP):
            b = g % 2
            pe.wait(bfree[b])
            for q in range(nb):
                m = pe.sig(TE.transpose, PSALL[:, b, q * P:(q + 1) * P], YT[:, (t0 + q) * P:(t0 + q + 1) * P],
                           ident[:, :])
            dv.wait(m)
            bfree[b] = y3_ok = dv.sig(V.tensor_copy, Y3[:, t0:t0 + nb, :],
                                      PSALL[:, b, 0:nb * P].rearrange("p (b d) -> p b d", b=nb))
        xp_ok = split3(Y3, xp, None, (y3_ok,), SL)
        bank_free = [y3_ok] * 8
        outs = {}
        late = None

        def store(item):
            it, mrow, fin = item
            ok = fin()
            sp.wait(ok)
            sp.dma(s_out[it % 2], nc.sync.dma_start, out[it * P:it * P + mrow, :], hb[0:mrow, it % 2, :])
            outs[it] = (s_out[it % 2], 16 * (it // 2 + 1))

        for it in range(T):
            m, mrow, view = spread(it, xp_ok, it % 4)
            s = it % 2
            hh = hb[0:mrow, s, :]
            dv.wait(m, outs.get(it - 2))
            r = dv.sig(V.tensor_reduce, hh, view, AX.X, ALU.add)
            bank_free[it % 4] = r
            dv.wait(r)
            r = dv.sig(V.tensor_tensor, hh, hh, AO3[0:mrow, it, :], ALU.add)
            _, fin = norm(hh, mrow, it, hh, r)
            if late is not None:
                store(late)
            late = (it, mrow, fin)
        store(late)
        sp.wait(outs[T - 1], outs[T - 2])
        sp.wait(AT_in)

        block = ctx.enter_context(nc.Block())

        @block.sync
        def _(eng):
            sp.emit(eng)

        @block.gpsimd
        def _(eng):
            gp.emit(eng)

        @block.scalar
        def _(eng):
            ac_.emit(eng)

        @block.vector
        def _(eng):
            dv.emit(eng)

        @block.tensor
        def _(eng):
            pe.emit(eng)


def kernel(x, adj, L0_gnn_t, L0_gnn_alpha, L0_gnn_beta, L1_gnn_W, L1_gnn_a):
    import numpy as np
    import concourse.bacc as bacc
    from concourse.bass_utils import run_bass_kernel_spmd as run

    nc = bacc.Bacc("TRN2", target_bir_lowering=False, num_devices=1)
    x, adj = np.asarray(x), np.asarray(adj)
    xr = np.zeros((NP, D), x.dtype)
    xr[:N] = x
    ar = np.zeros((NP, NP), adj.dtype)
    ar[:N, :N] = adj
    at = np.zeros((NP, N), adj.dtype)
    at[:N] = adj.T
    arrays = {
        "x": xr, "adj": ar, "adjT": at,
        "alpha": np.asarray(L0_gnn_alpha).reshape(1, 1), "beta": np.asarray(L0_gnn_beta).reshape(1, 1),
        "W": np.ascontiguousarray(L1_gnn_W), "a": np.ascontiguousarray(np.asarray(L1_gnn_a).reshape(2, D).T),
    }
    args = [nc.dram_tensor(f"in_{k}", v.shape, mybir.dt.from_np(v.dtype), kind="ExternalInput").ap()
            for k, v in arrays.items()]
    args.append(nc.dram_tensor("out_0", (N, D), F32, kind="ExternalOutput").ap())
    adj_resnorm2_kernel(nc, *args)
    r = run(nc, [{f"in_{k}": v for k, v in arrays.items()}], core_ids=[0])
    return r.results[0]["out_0"]
```

```python
from contextlib import ExitStack

import concourse.bass as bass
from concourse import mybir

P = 128
N = 2708
T = 22
NP = T * P
D = 128
LAST = N - (T - 1) * P
CH = [(c * 452, min(452, N - c * 452)) for c in range(6)]
SIMC = [(0, 1024), (1024, 1024), (2048, N - 2048)]
GRP = [(g * 4, min(4, T - g * 4)) for g in range(6)]
XS = 1024.0
SLOPE = 0.01
R1N = 11286
RW = 452
LN_EXP_SET = 6
WN = 4
TINY = 2.0 ** -64
LNZ = -40.0
LN_EPS = 1e-5
COS_EPS = 1e-8

ALU = mybir.AluOpType
ACT = mybir.ActivationFunctionType
AX = mybir.AxisListType
F32 = mybir.dt.float32
BF16 = mybir.dt.bfloat16
FP16 = mybir.dt.float16
U32 = mybir.dt.uint32
I32 = mybir.dt.int32


class Line:

    def __init__(self, sem):
        self.sem = sem
        self.n = 0
        self.items = []
        self.met = {}

    def wait(self, *marks):
        for mark in marks:
            if mark is None:
                continue
            sem, v = mark
            if self.met.get(id(sem), 0) < v:
                self.met[id(sem)] = v
                self.items.append(("wait", sem, v, None))

    def do(self, fn, *a, **k):
        self.items.append(("quiet", fn, a, k))

    def sig(self, fn, *a, **k):
        self.n += 1
        self.items.append(("sig", fn, a, k))
        return (self.sem, self.n)

    def dma(self, sem, fn, *a, **k):
        self.items.append(("dma", fn, a, (k, sem)))

    def either(self, flag, small, large):
        self.items.append(("either", flag, (small, large), self.n))
        self.n += len(large)
        return (self.sem, self.n)

    def branch(self, eng, steps, base, total):
        for i, (fn, a, k) in enumerate(steps):
            if i:
                eng.wait_ge(self.sem, base + i)
            fn(*a(), **k).then_inc(self.sem, 1 if i + 1 < len(steps) else total - i)

    def emit(self, eng):
        for kind, x, a, k in self.items:
            if kind == "wait":
                eng.wait_ge(x, a)
            elif kind == "either":
                with eng.If(x() == 0):
                    self.branch(eng, a[0], k, len(a[1]))
                with eng.Else():
                    self.branch(eng, a[1], k, len(a[1]))
            elif kind == "quiet":
                x(*a, **k)
            elif kind == "sig":
                x(*a, **k).then_inc(self.sem, 1)
            else:
                x(*a, **k[0]).then_inc(k[1], 16)


def adj_resnorm2_kernel(nc, x, adj, adjT, alpha, beta, W, a, out):
    with ExitStack() as ctx:
        def sb(name, shape, dt=F32):
            return ctx.enter_context(nc.sbuf_tensor(name, shape, dt))

        def sem(name):
            return ctx.enter_context(nc.semaphore(name))

        AT = sb("AT", [P, T, N], BF16)
        R1 = sb("R1", [P, R1N])
        X = sb("X", [P, NP])
        AO = sb("AO", [P, NP])
        XN = sb("XN", [P, NP])
        Wt = sb("Wt", [P, D])
        ident = sb("ident", [P, P])
        ac = sb("ac", [P, 2])[:, :]
        sm = sb("sm", [P, 16])
        st = sb("st", [P, 13, T])
        mx = sb("mx", [P, 2, 4])
        ln = sb("ln", [P, 2, 12])
        ring = sb("ring", [P, 6, RW])
        hb = ring[:, 0:2, 0:D]
        U = sb("U", [P, P], BF16)
        ones = sb("ones", [P, 1], BF16)
        rec = sb("rec", [P, T, 2])
        idx = sb("idx", [P, 4, T], U32)
        mk = sb("mk", [P, T])
        win = sb("win", [1, 4 * T], I32)
        winf = ring[0:1, 5, 0:4 * T]
        tie = ring[:, 3, 0:P].bitcast(BF16).rearrange("p (q j) -> p q j", q=2)

        PSALL = ctx.enter_context(nc.psum_tensor("PSALL", [P, 8, 512], F32))

        X3 = X[:, :].rearrange("p (t d) -> p t d", t=T)
        AO3 = AO[:, :].rearrange("p (t d) -> p t d", t=T)
        Ab = [R1[:, s * NP:(s + 1) * NP] for s in range(3)]
        junk = R1[:, 3 * NP:3 * NP + NP // 2].bitcast(BF16)
        ET = [R1[:, 3 * NP + NP // 2 + s * 512:3 * NP + NP // 2 + (s + 1) * 512].rearrange("p (b i) -> p b i", b=4)
              for s in range(2)]
        xnh = XN[:, 0:NP // 2].bitcast(FP16)
        xnl = XN[:, NP // 2:NP].bitcast(FP16)
        xp = R1[:, 0:3 * NP // 2].bitcast(BF16).rearrange("p (t c d) -> p t c d", t=T, c=3)
        XWs = XN[:, :].rearrange("p (t d) -> p t d", t=T)
        srows = XN[0:2, :]
        rb = R1[:, 0:NP]
        cb = X[:, :]
        XWn = R1[:, NP:NP + T * (D + 1)].rearrange("p (t d) -> p t d", t=T)
        x1T = R1[:, 5654:5654 + NP]
        XWT = R1[:, 8470:8470 + NP]
        Cb = [R1[:, 5654 + q * 1408:5654 + (q + 1) * 1408].bitcast(BF16) for q in range(4)]
        W3 = [R1[:, NP + q * 1408:NP + (q + 1) * 1408].bitcast(BF16) for q in range(2)]
        zt = R1[:, 2 * NP:3 * NP]
        den_f = [R1[:, NP:2 * NP], R1[:, 2 * NP:3 * NP]]
        den_b = [v.bitcast(BF16).rearrange("p (t c j) -> p t c j", t=T, c=2) for v in den_f]
        fw = R1[:, 3 * NP:3 * NP + WN * P]
        tab = R1[:, 3 * NP + WN * P:3 * NP + WN * P + N // 2].bitcast(BF16)
        EHL = [AO[:, q * 1408:(q + 1) * 1408].bitcast(BF16) for q in range(2)]
        rest = 3 * NP + WN * P + N // 2
        tZ = [ring[:, q, :] for q in range(3)] + [R1[:, rest + q * RW:rest + (q + 1) * RW] for q in range(2)]
        tL = [ring[:, 3 + q, :] for q in range(3)]
        bcol, sig, eal, one = sm[:, 0:1], sm[:, 1:2], sm[:, 2:3], sm[:, 3:4]
        braw, araw = sm[:, 4:5], sm[:, 5:6]
        epsc = sm[:, 6:7]
        half, mhalf = sm[:, 7:8], sm[:, 8:9]
        tiny, ref, is0 = sm[:, 9:10], sm[:, 10:11], sm[:, 11:12]
        sq, nrm, rn, deg, dis, rs, rrs, scol, srow, cs, rsrt, wu, wl = (st[:, i, :] for i in range(13))

        s_pe, s_dv, s_ac, s_gp = sem("s_pe"), sem("s_dv"), sem("s_ac"), sem("s_gp")
        s_x, s_w, s_const = sem("s_x"), sem("s_w"), sem("s_const")
        s_A = [sem(f"s_A{i}") for i in range(3)]
        s_AT = sem("s_AT")
        s_ATd, s_x1, s_sd, s_sb, s_sc, s_sr, s_rt, s_ct, s_AS, s_Yd, s_Yg = (
            sem(n) for n in ("s_ATd", "s_x1", "s_sd", "s_sb", "s_sc", "s_sr", "s_rt", "s_ct", "s_AS", "s_Yd", "s_Yg"))
        s_x1b, s_xw = sem("s_x1b"), sem("s_xw")
        s_out = [sem(f"s_out{i}") for i in range(2)]

        ATd = nc.dram_tensor("ATd", (NP, N), BF16, kind="Internal").ap()
        x1d = nc.dram_tensor("x1d", (NP, D), F32, kind="Internal").ap()
        sd = nc.dram_tensor("sd", (2, NP), F32, kind="Internal").ap()
        XWd = nc.dram_tensor("XWd", (NP, D + 1), F32, kind="Internal").ap()
        RKd = nc.dram_tensor("RKd", (NP, 2), F32, kind="Internal").ap()
        Yd = nc.dram_tensor("Yd", (NP, D), F32, kind="Internal").ap()

        pe, dv, ac_, gp, sp = Line(s_pe), Line(s_dv), Line(s_ac), Line(s_gp), Line(None)
        V, S, G, TE = nc.vector, nc.scalar, nc.gpsimd, nc.tensor

        sp.dma(s_x, nc.sync.dma_start, X3, x.rearrange("(t p) d -> p t d", p=P))
        x_in = (s_x, 16)
        small = [(Wt[:, :], W), (ac, a),
                 (braw, beta.broadcast_to([P, 1])), (araw, alpha.broadcast_to([P, 1]))]
        A_in = {}
        A_free = {}

        def load_A(it):
            s = it % 3
            if it >= 3:
                sp.wait(A_free[it - 3])
            sp.dma(s_A[s], nc.sync.dma_start, Ab[s], adj[it * P:(it + 1) * P, :])
            A_in[it] = (s_A[s], 16 * (it // 3 + 1))

        load_A(0)
        for dst, src in small:
            sp.dma(s_w, nc.sync.dma_start, dst, src)
        w_in = (s_w, 16 * len(small))
        load_A(1)
        load_A(2)

        m = gp.sig(G.memset, ident[:, :], 0.0)
        gp.wait(m)
        id_ok = gp.sig(G.affine_select, out=ident[:, :], in_=ident[:, :], compare_op=ALU.not_equal, fill=1.0,
                       base=0, pattern=[[-1, P]], channel_multiplier=1)
        gp.sig(G.memset, half, 0.5)
        pc_ok = gp.sig(G.memset, mhalf, -0.5)
        gp.sig(G.memset, tiny, TINY)
        gp.sig(G.memset, ones[:, :], 1.0)
        gp.sig(G.memset, sm[:, 12:16], 0.0)
        gp.sig(G.memset, U[:, :], 1.0)
        m = gp.sig(G.iota, idx[:, 0, :].bitcast(I32), pattern=[[P, T]], base=0, channel_multiplier=1)
        gp.wait(m)
        gp.sig(G.affine_select, out=U[:, :], in_=U[:, :], compare_op=ALU.is_gt, fill=0.0,
               base=0, pattern=[[1, P]], channel_multiplier=-1)
        gp.wait((s_gp, gp.n))
        m = gp.sig(G.memset, sm[0:1, 12:13], 1.0)
        gp.wait(m)
        m = gp.sig(G.memset, sm[0:T, 13:14], 1.0)
        gp.wait(m)
        cst_ok = gp.sig(G.memset, sm[32:32 + T, 14:15], 1.0)
        gp.wait(cst_ok)
        for kt in range(T):
            gp.dma(s_AT, G.dma_start, AT[:, kt, :], adjT[kt * P:(kt + 1) * P, :])
        AT_in = (s_AT, 16 * T)

        xx = AO3
        dv.wait(x_in)
        m = dv.sig(V.tensor_tensor, xx, X3, X3, ALU.mult)
        dv.wait(m)
        m = dv.sig(V.tensor_reduce, sq, xx, AX.X, ALU.add)
        gp.wait(m, pc_ok)
        m = gp.sig(G.tensor_tensor, nrm, sq, half.broadcast_to([P, T]), ALU.pow)
        dv.wait(m)
        m = dv.sig(V.tensor_scalar, nrm, nrm, COS_EPS, 1.0 / XS, ALU.max, ALU.mult)
        dv.wait(m)
        m = dv.sig(V.reciprocal, rn, nrm)
        dv.wait(m)
        xn_ok = dv.sig(V.tensor_tensor, AO3, X3, rn.unsqueeze(2).broadcast_to([P, T, D]), ALU.mult)
        pe.wait(xn_ok, id_ok)
        free = [None, None]
        split = None
        for g, (t0, nb) in enumerate(GRP):
            b = g % 2
            pe.wait(free[b])
            for q in range(nb):
                m = pe.sig(TE.transpose, PSALL[:, b, q * P:(q + 1) * P], AO3[:, t0 + q, :], ident[:, :])
            w = nb * P
            c0 = t0 * P
            dv.wait(m)
            h = dv.sig(V.tensor_copy, xnh[:, c0:c0 + w], PSALL[:, b, 0:w])
            dv.wait(h)
            split = free[b] = dv.sig(V.tensor_tensor, xnl[:, c0:c0 + w], PSALL[:, b, 0:w], xnh[:, c0:c0 + w],
                                     ALU.subtract)
        ao_free = m
        ac_.wait(w_in)
        e = ac_.sig(S.activation, eal, araw, ACT.Exp, scale=-1.0)
        dv.wait(e)
        m = dv.sig(V.tensor_scalar, eal, eal, 1.0, None, ALU.add)
        dv.wait(m)
        sig_ok = dv.sig(V.reciprocal, sig, eal)
        dv.wait(w_in)
        bc_ok = dv.sig(V.tensor_scalar, bcol, braw, 1.0 / (XS * XS), None, ALU.mult)

        ps_free = [split, split, split, split]
        pair = 0
        exp_done = {}
        sub_ao = {}

        def sim(it):
            nonlocal pair
            s = it % 3
            ac_.wait(A_in[it])
            d = ac_.sig(S.activation, junk, Ab[s], ACT.Copy, accum_out=deg[:, it:it + 1])
            if it >= 2:
                dv.wait(exp_done[it - 2])
            for c, (c0, w) in enumerate(SIMC):
                b = pair % 2
                pair += 1
                pe.wait(ps_free[b])
                for o in range(0, w, 512):
                    ww = min(512, w - o)
                    dst = PSALL[:, 2 * b + o // 512, 0:ww]
                    k = 0
                    for lh, rh in ((xnh, xnh), (xnh, xnl), (xnl, xnh)):
                        args = (dst, lh[:, it * P:(it + 1) * P], rh[:, c0 + o:c0 + o + ww])
                        kw = dict(start=(k == 0), stop=(k == 2))
                        if k == 2 and o + 512 >= w:
                            m = pe.sig(TE.matmul, *args, **kw)
                        else:
                            pe.do(TE.matmul, *args, **kw)
                        k += 1
                dv.wait(m, A_in[it], d, bc_ok)
                src = PSALL[:, 2 * b:2 * b + 2, :].rearrange("p b n -> p (b n)")[:, 0:w]
                ps_free[b] = l = dv.sig(V.tensor_tensor_reduce, out=Ab[s][:, c0:c0 + w], in0=src,
                                        in1=Ab[s][:, c0:c0 + w], scale=bcol, scalar=-3.4e38,
                                        op0=ALU.mult, op1=ALU.max, accum_out=mx[:, it % 2, c:c + 1])
            dv.wait(l)
            r = dv.sig(V.tensor_reduce, mx[:, it % 2, 3:4], mx[:, it % 2, 0:3], AX.X, ALU.max)
            dv.wait(r)
            r = dv.sig(V.tensor_scalar, mx[:, it % 2, 3:4], mx[:, it % 2, 3:4], -1.0, None, ALU.mult)
            ac_.wait(r)
            exp_done[it] = ac_.sig(S.activation, Ab[s][:, 0:N], Ab[s][:, 0:N], ACT.Exp, bias=mx[:, it % 2, 3:4],
                                   accum_out=rs[:, it:it + 1])

        pt_free = [split, split]
        et_free = [None, None]
        po_free = [None, None]
        tg = 0

        def attend(it):
            nonlocal tg
            s = it % 3
            pe.wait(exp_done[it])
            po = PSALL[:, 6 + it % 2, 0:D]
            pend = None

            def mm(t0, nb, e, ok):
                pe.wait(ok)
                if t0 == 0:
                    pe.wait(po_free[it % 2])
                for q in range(nb):
                    args = (po, ET[e][:, q, :], X3[:, t0 + q, :])
                    kw = dict(start=(t0 + q == 0), stop=(t0 + q == T - 1))
                    if q == nb - 1:
                        et_free[e] = pe.sig(TE.matmul, *args, **kw)
                    else:
                        pe.do(TE.matmul, *args, **kw)

            for t0, nb in GRP:
                b = tg % 2
                pe.wait(pt_free[b])
                for q in range(nb):
                    src = Ab[s][:, (t0 + q) * P:(t0 + q + 1) * P]
                    dst = PSALL[:, 4 + b, q * P:(q + 1) * P]
                    if q == nb - 1:
                        m = pe.sig(TE.transpose, dst, src, ident[:, :])
                    else:
                        pe.do(TE.transpose, dst, src, ident[:, :])
                if pend is not None:
                    mm(*pend)
                ev = dv if tg % 2 else ac_
                ev.wait(m, et_free[b])
                dstv = ET[b][:, 0:nb, :].rearrange("p b i -> p (b i)")
                srcv = PSALL[:, 4 + b, 0:nb * P]
                if tg % 2:
                    ok = dv.sig(V.tensor_copy, dstv, srcv)
                else:
                    ok = ac_.sig(S.activation, dstv, srcv, ACT.Copy)
                pt_free[b] = ok
                pend = (t0, nb, b, ok)
                tg += 1
            A_free[it] = m
            mm(*pend)
            att = et_free[pend[2]]
            dv.wait(exp_done[it])
            r = dv.sig(V.reciprocal, rrs[:, it:it + 1], rs[:, it:it + 1])
            dv.wait(r, att, ao_free)
            po_free[it % 2] = sub_ao[it] = dv.sig(V.scalar_tensor_tensor, AO3[:, it, :], po, rrs[:, it:it + 1],
                                                  X3[:, it, :], ALU.mult, ALU.subtract)

        sim(0)
        for it in range(T):
            if it + 1 < T:
                sim(it + 1)
            attend(it)
            if it + 3 < T:
                load_A(it + 3)
            if it == 12:
                sp.wait(AT_in)
                for q in range(2):
                    sp.dma(s_ATd, nc.sync.dma_start,
                           ATd[q * 11 * P:(q + 1) * 11 * P, :].rearrange("(t p) n -> p t n", p=P),
                           AT[:, q * 11:(q + 1) * 11, :])

        def split3(src3, dst, tmp, first, slices):
            done = []
            for (t0, nt) in slices:
                sl = src3[:, t0:t0 + nt, :]
                dv.wait(*first)
                h = dv.sig(V.tensor_copy, dst[:, t0:t0 + nt, 0, :], sl)
                dv.wait(h)
                r = dv.sig(V.tensor_tensor, sl, sl, dst[:, t0:t0 + nt, 0, :], ALU.subtract)
                dv.wait(r)
                h = dv.sig(V.tensor_copy, dst[:, t0:t0 + nt, 1, :], sl)
                dv.wait(h)
                done.append(dv.sig(V.tensor_tensor, dst[:, t0:t0 + nt, 2, :], sl, dst[:, t0:t0 + nt, 1, :],
                                   ALU.subtract))
            return done

        SL = [(0, 6), (6, 6), (12, 6), (18, 4)]
        xd3 = R1[:, 3 * NP:4 * NP].rearrange("p (t d) -> p t d", t=T)
        att_end = et_free[(tg - 1) % 2]
        dv.wait(att_end)
        m = dv.sig(V.tensor_scalar, dis, deg, 1.0, None, ALU.max)
        gp.wait(m)
        m = gp.sig(G.tensor_tensor, dis, dis, mhalf.broadcast_to([P, T]), ALU.pow)
        dv.wait(m)
        m = dv.sig(V.tensor_tensor, xd3, X3, dis.unsqueeze(2).broadcast_to([P, T, D]), ALU.mult)
        xp_ok = split3(xd3, xp, None, (m,), SL)

        bank_free = [sub_ao[T - 1]] * 8
        sq_dve = sub_ao[T - 1]
        hb_free = [None, None]
        x1_ok = {}

        def spread(it, parts_ok, bank, xp):
            mrow = P if it < T - 1 else LAST
            pe.wait(bank_free[bank])
            for jt in range(T):
                for (t0, nt), ok in zip(SL, parts_ok):
                    if jt == t0:
                        pe.wait(ok)
                args = (PSALL[0:mrow, bank, 0:3 * D], AT[:, jt, it * P:it * P + mrow],
                        xp[:, jt, :, :].rearrange("p c d -> p (c d)"))
                kw = dict(start=(jt == 0), stop=(jt == T - 1))
                if jt == T - 1:
                    m = pe.sig(TE.matmul, *args, **kw)
                else:
                    pe.do(TE.matmul, *args, **kw)
            return m, mrow, PSALL[0:mrow, bank, 0:3 * D].rearrange("p (c d) -> p d c", c=3)

        def norm(h, mrow, it, dst, ok):
            s = it % 2
            dv.wait(ok)
            b = dv.sig(V.bn_stats, ln[0:mrow, s, 0:6], h)
            dv.wait(b)
            b = dv.sig(V.bn_aggr, ln[0:mrow, s, 6:8], ln[0:mrow, s, 0:6])
            dv.wait(b)
            b = dv.sig(V.tensor_scalar, ln[0:mrow, s, 8:9], ln[0:mrow, s, 7:8], LN_EPS, None, ALU.add)
            gp.wait(b)
            b = gp.sig(G.tensor_tensor, ln[0:mrow, s, 9:10], ln[0:mrow, s, 8:9], mhalf[0:mrow, :], ALU.pow)
            return b, (lambda: (dv.wait(b), dv.sig(V.tensor_scalar, dst, h, ln[0:mrow, s, 6:7],
                                                   ln[0:mrow, s, 9:10], ALU.subtract, ALU.mult))[1])

        pe.wait(AT_in)
        late = None
        gz = gp.sig(G.memset, hb[:, :, :], 0.0)

        def layer0_tail(it, m, mrow, view):
            s = it % 2
            hh = hb[0:mrow, s, :]
            dv.wait(m, hb_free[s], sig_ok, gz)
            r = dv.sig(V.tensor_reduce, hh, view, AX.X, ALU.add)
            bank_free[it % 4] = r
            dv.wait(r)
            r = dv.sig(V.scalar_tensor_tensor, hh, hh, dis[0:mrow, it:it + 1], X3[0:mrow, it, :],
                       ALU.mult, ALU.subtract)
            dv.wait(r)
            r = dv.sig(V.scalar_tensor_tensor, hh, AO3[0:mrow, it, :], sig[0:mrow, :], hh, ALU.mult, ALU.add)
            dv.wait(r)
            r = dv.sig(V.tensor_tensor, hh, hh, X3[0:mrow, it, :], ALU.add)
            return norm(hh, mrow, it, AO3[0:mrow, it, :], r)

        def flush(item):
            it, fin = item
            if it == T - 1:
                z = dv.sig(V.memset, AO3[:, it, :], 0.0)
                dv.wait(z)
            x1_ok[it] = hb_free[it % 2] = fin()

        for it in range(T):
            m, mrow, view = spread(it, xp_ok, it % 4, xp)
            if it == T - 1:
                flush(late)
                late = None
            _, fin = layer0_tail(it, m, mrow, view)
            if late is not None:
                flush(late)
            late = (it, fin)
        flush(late)

        p2_end = m
        sp.wait(x1_ok[T - 1])
        sp.dma(s_x1, nc.sync.dma_start, x1d.rearrange("(t p) d -> p t d", p=P), AO3)
        bfree = dict((b, x1_ok[T - 1]) for b in range(8))
        xwn_ok = srow_ok = None
        dv.wait(p2_end)
        for g, (t0, nb) in enumerate(GRP):
            c0, w = t0 * P, nb * P
            b = g % 2
            pe.wait(x1_ok[t0 + nb - 1], bfree[b])
            for q in range(nb):
                m = pe.sig(TE.transpose, PSALL[:, b, q * P:(q + 1) * P], AO3[:, t0 + q, :], ident[:, :])
            dv.wait(m)
            ok = bfree[b] = dv.sig(V.tensor_copy, x1T[:, c0:c0 + w], PSALL[:, b, 0:w])
            b = 2 + g % 2
            pe.wait(ok, bfree[b])
            m = pe.sig(TE.matmul, PSALL[:, b, 0:w], Wt[:, :], x1T[:, c0:c0 + w], start=True, stop=True)
            ac_.wait(m)
            ok = bfree[b] = ac_.sig(S.activation, XWT[:, c0:c0 + w], PSALL[:, b, 0:w], ACT.Copy)
            b = 4 + g % 2
            pe.wait(bfree[b])
            for q in range(nb):
                m = pe.sig(TE.matmul, PSALL[:, b, q * P:(q + 1) * P], x1T[:, c0 + q * P:c0 + (q + 1) * P], Wt[:, :],
                           start=True, stop=True)
            dv.wait(m)
            xwn_ok = bfree[b] = dv.sig(V.tensor_copy, XWn[:, t0:t0 + nb, 0:D],
                                       PSALL[:, b, 0:w].rearrange("p (b d) -> p b d", b=nb))
            b = 6 + g % 2
            pe.wait(ok, bfree[b])
            m = pe.sig(TE.matmul, PSALL[0:2, b, 0:w], ac, XWT[:, c0:c0 + w], start=True, stop=True)
            ac_.wait(m)
            srow_ok = bfree[b] = ac_.sig(S.activation, srows[:, c0:c0 + w], PSALL[0:2, b, 0:w], ACT.Copy)
        xw_end = m
        sp.wait(srow_ok)
        sp.dma(s_sd, nc.sync.dma_start, sd, srows)
        sd_ok = (s_sd, 16)
        sp.wait(sd_ok, xwn_ok)
        ac_.wait(sd_ok)
        sp.dma(s_sb, nc.sync.dma_start, rb, sd[1:2, :].broadcast_to([P, NP]))
        sp.dma(s_sc, nc.sync.dma_start, cb, sd[0:1, :].broadcast_to([P, NP]))
        ac_.dma(s_sb, nc.scalar.dma_start, srow.unsqueeze(2), sd[1:2, :].rearrange("o (t p u) -> (o p) t u", p=P, u=1),
                allow_slow_non_contiguous=True)
        ac_.dma(s_sc, nc.scalar.dma_start, scol.unsqueeze(2), sd[0:1, :].rearrange("o (t p u) -> (o p) t u", p=P, u=1),
                allow_slow_non_contiguous=True)
        view_ok = {"r": (s_sb, 32), "c": (s_sc, 32)}

        c_free = [None] * 4
        row_read = xw_end
        cn = 0
        rank_ok = {}
        for which, bc, per, bank, slot in (("r", rb, srow, 6, 1), ("c", cb, scol, 7, 2)):
            for lt in range(T):
                q = cn % 4
                cn += 1
                lo, hi = lt * P, (lt + 1) * P
                rows = P if lt < T - 1 else LAST
                sc1 = per[:, lt:lt + 1]
                C = Cb[q]
                dv.wait(view_ok[which], c_free[q], xw_end, cst_ok)
                e = dv.sig(V.scalar_tensor_tensor, tie[:, q % 2, :], bc[:, lo:hi], sc1, U[:, :],
                           ALU.is_equal, ALU.mult)
                if lt:
                    dv.sig(V.tensor_scalar, C[:, 0:lo], bc[:, 0:lo], sc1, None, ALU.is_gt)
                if lt < T - 1:
                    dv.sig(V.tensor_scalar, C[:, hi:NP], bc[:, hi:NP], sc1, None, ALU.is_ge)
                dv.wait(e)
                c_ok = dv.sig(V.scalar_tensor_tensor, C[:, lo:hi], bc[:, lo:hi], sc1, tie[:, q % 2, :],
                              ALU.is_gt, ALU.add)
                pe.wait(c_ok)
                if lt == 0:
                    pe.wait(rank_ok.get("row", bfree[4]), *bfree.values())
                for c, (c0, w) in enumerate(CH):
                    m = pe.sig(TE.matmul, PSALL[0:1, c, 0:w], ones[0:rows, :], C[0:rows, c0:c0 + w],
                               start=(lt == 0), stop=(lt == T - 1))
                c_free[q] = m
            ac_.wait(m, row_read, sd_ok)
            for c, (c0, w) in enumerate(CH):
                m = ac_.sig(S.activation, XN[0:1, c0:c0 + w], PSALL[0:1, c, 0:w], ACT.Copy)
            rank_ok["row"] = m
            pe.wait(m, cst_ok)
            for t in range(T):
                rows = P if t < T - 1 else LAST
                m = pe.sig(TE.matmul, PSALL[0:rows, bank, t:t + 1], XN[0:1, t * P:t * P + rows], sm[0:1, 12:13],
                           start=True, stop=True)
            row_read = m
            dv.wait(m)
            z = dv.sig(V.tensor_copy, idx[:, slot, T - 1:T], idx[:, 0, T - 1:T])
            dv.sig(V.tensor_copy, idx[:, slot, 0:T - 1], PSALL[:, bank, 0:T - 1])
            dv.wait(z)
            rank_ok[which] = dv.sig(V.tensor_copy, idx[0:LAST, slot, T - 1:T], PSALL[0:LAST, bank, T - 1:T])
            if which == "r":
                e = dv.sig(V.tensor_copy, rec[:, :, 0].bitcast(U32), idx[:, 0, :])
                e = dv.sig(V.tensor_copy, rec[:, :, 1], srow)
            else:
                e = dv.sig(V.tensor_copy, XWn[:, :, D], scol)
            gp.wait(e, rank_ok[which])
            for t in range(T):
                if which == "r":
                    gp.dma(s_sr, G.indirect_dma_start, out=RKd, out_offset=bass.IndirectOffsetOnAxis(
                        ap=idx[:, slot, t:t + 1], axis=0), in_=rec[:, t, :], in_offset=None)
                else:
                    gp.dma(s_sr, G.indirect_dma_start, out=XWd, out_offset=bass.IndirectOffsetOnAxis(
                        ap=idx[:, slot, t:t + 1], axis=0), in_=XWn[:, t, :], in_offset=None)
            if which == "r":
                gp.wait((s_sr, 16 * T))
                gp.dma(s_rt, G.dma_start, rec[:, :, :], RKd.rearrange("(t p) c -> p t c", p=P))
                perm_ok = (s_rt, 16)
                gp.wait(perm_ok, p2_end, (s_ATd, 32))
                e = gp.sig(G.tensor_copy, idx[:, 3, :], rec[:, :, 0].bitcast(U32))
                gp.wait(e)
                for t in range(T):
                    gp.dma(s_AS, G.indirect_dma_start, out=AT[:, t, :], out_offset=None, in_=ATd,
                           in_offset=bass.IndirectOffsetOnAxis(ap=idx[:, 3, t:t + 1], axis=0))
                rs_ok = dv_rs = None
        gp.wait((s_sr, 32 * T))
        gp_xw = (s_sr, 32 * T)
        sp.wait(gp_xw, row_read)
        sp.dma(s_ct, nc.sync.dma_start, cs.unsqueeze(2), XWd[:, D:D + 1].rearrange("(t p) u -> p t u", p=P),
               allow_slow_non_contiguous=True)
        cs_ok = (s_ct, 16)
        sp.dma(s_xw, nc.sync.dma_start, XWs, XWd[:, 0:D].rearrange("(t p) d -> p t d", p=P))
        XWs_ok = (s_xw, 16)

        onesf = ring[:, 0, 0:P]
        e = gp.sig(G.memset, onesf, 1.0)
        dv.wait(cs_ok, c_free[0], c_free[1], c_free[2], c_free[3])
        m = dv.sig(V.tensor_tensor, zt.rearrange("p (t j) -> p t j", t=T),
                   ident[:, :].unsqueeze(1).broadcast_to([P, T, P]), cs.unsqueeze(2).broadcast_to([P, T, P]), ALU.mult)
        pe.wait(m, e)
        bfree = {0: rank_ok["c"], 1: rank_ok["c"]}
        for g, (t0, nb) in enumerate(GRP):
            b = g % 2
            pe.wait(bfree[b])
            m = pe.sig(TE.matmul, PSALL[:, b, 0:nb * P], onesf, zt[:, t0 * P:(t0 + nb) * P], start=True, stop=True)
            dv.wait(m)
            bfree[b] = cb_ok = dv.sig(V.tensor_copy, cb[:, t0 * P:(t0 + nb) * P], PSALL[:, b, 0:nb * P])
        zt_free = m

        rs4 = ring[:, 1, 0:P]
        e = gp.sig(G.memset, rs4, 0.0)
        dv.wait(perm_ok, e)
        r_ok = dv.sig(V.tensor_copy, rsrt, rec[:, :, 1])
        for q in range(4):
            m = dv.sig(V.tensor_copy, rs4[:, 32 * q:32 * q + T], rec[:, :, 1])
        pe.wait(m, r_ok, rank_ok["c"])
        m = pe.sig(TE.transpose, PSALL[:, 2, 0:P], rs4, ident[:, :])
        selr = ring[:, 2, 0:P]
        e = gp.sig(G.memset, selr, 0.0)
        gp.wait(e)
        e = gp.sig(G.memset, selr[0:1, :], 1.0)
        pe.wait(e)
        m2 = pe.sig(TE.matmul, PSALL[:, 3, 0:T], selr, rsrt, start=True, stop=True)
        dv.wait(m, m2)
        ref_ok = dv.sig(V.tensor_copy, ref, PSALL[:, 2, 0:1])
        rmax_ok = dv.sig(V.tensor_reduce, is0, PSALL[:, 2, 0:P], AX.X, ALU.max)
        dv.wait(ref_ok, rmax_ok, cb_ok)
        cb3 = cb[:, :].rearrange("p (t j) -> p t j", t=T)
        for q in range(4):
            a0 = 32 * q
            if q % 2 == 0:
                m = dv.sig(V.tensor_scalar, mk[a0:a0 + 32, :], cb3[a0:a0 + 32, :, 0], ref[a0:a0 + 32, :], 0.0,
                           ALU.add, ALU.is_gt)
            else:
                dv.sig(V.tensor_scalar, mk[a0:a0 + 32, 0:T - 1], cb3[a0:a0 + 32, 0:T - 1, P - 1],
                       is0[a0:a0 + 32, :], 0.0, ALU.add, ALU.is_le)
                m = dv.sig(V.tensor_scalar, mk[a0:a0 + 32, T - 1:T], cb3[a0:a0 + 32, T - 1:T, LAST - 1],
                           is0[a0:a0 + 32, :], 0.0, ALU.add, ALU.is_le)
        mk_ok = m
        pe.wait(mk_ok)
        m = pe.sig(TE.matmul, PSALL[0:1, 4, 0:T], sm[:, 14:15], mk[:, :], start=True, stop=True)
        m2 = pe.sig(TE.matmul, PSALL[0:1, 5, 0:T], sm[:, 13:14], mk[:, :], start=True, stop=True)
        dv.wait(m, m2)
        lof, hif, bf, ff = (winf[0:1, q * T:(q + 1) * T] for q in range(4))
        a1 = dv.sig(V.tensor_copy, lof, PSALL[0:1, 4, 0:T])
        a2 = dv.sig(V.tensor_scalar, hif, PSALL[0:1, 5, 0:T], -1.0, float(T), ALU.mult, ALU.add)
        dv.wait(a1, a2)
        dv.sig(V.tensor_scalar, bf, lof, float(T - WN), None, ALU.min)
        a1 = dv.sig(V.tensor_tensor, ff, hif, lof, ALU.subtract)
        dv.wait(a1)
        a1 = dv.sig(V.tensor_scalar, ff, ff, WN + 0.5, None, ALU.is_gt)
        dv.wait(a1)
        win_ok = dv.sig(V.tensor_copy, win[0:1, :], winf[0:1, :])
        r = dv.sig(V.tensor_tensor, wl, rsrt, PSALL[:, 3, 0:T], ALU.subtract)
        ac_.wait(r)
        m = ac_.sig(S.activation, wu, wl, ACT.Exp)
        ac_.wait(m)
        w_ok = ac_.sig(S.activation, wl, wl, ACT.Exp, scale=SLOPE)
        gp.wait(gp_xw)
        e = gp.sig(G.memset, R1[:, NP:2 * NP], 0.0)
        dv.wait(w_ok, e)
        for q in range(4):
            src = wu if q % 2 == 0 else wl
            cols = slice(32 * q, 32 * q + (T - 1) * (P + 1) + 1, P + 1)
            h = dv.sig(V.tensor_copy, W3[0][:, cols], src)
            dv.wait(h)
            wt_ok = dv.sig(V.tensor_tensor, W3[1][:, cols], src, W3[0][:, cols], ALU.subtract)
        dv.wait(zt_free)
        m = dv.sig(V.tensor_scalar, zt, cb[:, :], ref, None, ALU.add)
        dv.wait(m)
        m = dv.sig(V.scalar_tensor_tensor, zt, zt, SLOPE, zt, ALU.mult, ALU.max)
        ac_.wait(m)
        m = ac_.sig(S.activation, zt, zt, ACT.Exp)
        dv.wait(m, (s_x1, 16), xw_end)
        m = dv.sig(V.tensor_tensor, zt.rearrange("p (t j) -> p t j", t=T), zt.rearrange("p (t j) -> p t j", t=T),
                   mk[:, :].unsqueeze(2).broadcast_to([P, T, P]), ALU.mult)
        ac_.wait(m, (s_x1, 16))
        h = ac_.sig(S.activation, EHL[0], zt, ACT.Copy)
        dv.wait(h)
        E_ok = dv.sig(V.tensor_tensor, EHL[1], zt, EHL[0], ALU.subtract)

        pe.wait(wt_ok, win_ok, w_ok)
        for t in range(T):
            if t == 0:
                pe.wait((s_AS, 16 * T))
            for c, (c0, w) in enumerate(CH):
                for q in range(2):
                    args = (PSALL[:, c, 0:w], W3[q][:, t * P:(t + 1) * P], AT[:, t, c0:c0 + w])
                    m = pe.sig(TE.matmul, *args, start=(t == 0 and q == 0), stop=(t == T - 1 and q == 1))
        w3_free = m
        dv.wait(m)
        for c, (c0, w) in enumerate(CH):
            h = dv.sig(V.tensor_copy, tab[:, c0:c0 + w], PSALL[:, c, 0:w])
            dv.wait(h)
            tab_ok = dv.sig(V.tensor_tensor, tab[64:128, c0:c0 + w], PSALL[64:128, c, 0:w], tab[64:128, c0:c0 + w],
                            ALU.subtract)

        den_ok = {}
        den_free = {}
        den_at = {}
        vreg, areg, preg = {}, {}, {}

        def window(e, reg):
            def load(jt):
                reg["lo"] = e.value_load(win[0:1, jt:jt + 1], min_val=0, max_val=T)
                reg["hi"] = e.value_load(win[0:1, T + jt:T + jt + 1], min_val=0, max_val=T)
            return load

        def place(e, reg):
            def load(jt):
                reg["base"] = e.value_load(win[0:1, 2 * T + jt:2 * T + jt + 1], min_val=0, max_val=T - WN)
                reg["wide"] = e.value_load(win[0:1, 3 * T + jt:3 * T + jt + 1], min_val=0, max_val=1)
            return load

        def den(jt, stage):
            s = (jt + 1) % 2
            f3 = fw.rearrange("p (t j) -> p t j", t=WN)
            d3 = den_f[s].rearrange("p (t j) -> p t j", t=T)
            cbj = cb3[:, jt, :].unsqueeze(1)
            hi_, lo_ = den_b[s][:, :, 0, :], den_b[s][:, :, 1, :]

            def now(*a):
                return lambda: a

            def at(part):
                return lambda reg: part[:, bass.ds(reg["base"], WN), :]

            if stage == 0:
                dv.wait(win_ok, cb_ok, r_ok, E_ok, w3_free if jt == 1 else None, den_free.get(jt - 2))
                dv.do(place(V, vreg), jt)
                den_at[jt, 0] = dv.either(
                    lambda: vreg["wide"],
                    [(V.tensor_tensor, lambda: (f3, cbj.broadcast_to([P, WN, P]),
                                                rsrt[:, bass.ds(vreg["base"], WN)].unsqueeze(2).broadcast_to([P, WN, P]),
                                                ALU.add), {}),
                     (V.scalar_tensor_tensor, now(fw, fw, SLOPE, fw, ALU.mult, ALU.max), {})],
                    [(V.tensor_tensor, now(d3, cbj.broadcast_to([P, T, P]), rsrt.unsqueeze(2).broadcast_to([P, T, P]),
                                           ALU.add), {}),
                     (V.scalar_tensor_tensor, now(den_f[s], den_f[s], SLOPE, den_f[s], ALU.mult, ALU.max), {})])
            elif stage == 1:
                ac_.wait(win_ok, den_at[jt, 0])
                ac_.do(place(S, areg), jt)
                den_at[jt, 1] = ac_.either(
                    lambda: areg["wide"],
                    [(S.activation, now(fw, fw, ACT.Exp), {})],
                    [(S.activation, now(den_f[s], den_f[s], ACT.Exp), {})])
            else:
                dv.wait(den_at[jt, 1])
                wide = []
                for t0, nb in GRP:
                    f = f3[:, 0:nb, :]
                    wide += [(V.tensor_copy, now(f, d3[:, t0:t0 + nb, :]), {}),
                             (V.tensor_copy, now(hi_[:, t0:t0 + nb, :], f), {}),
                             (V.tensor_tensor, now(lo_[:, t0:t0 + nb, :], f, hi_[:, t0:t0 + nb, :], ALU.subtract), {})]
                den_ok[jt] = dv.either(
                    lambda: vreg["wide"],
                    [(V.tensor_copy, lambda: (at(hi_)(vreg), f3), {}),
                     (V.tensor_tensor, lambda: (at(lo_)(vreg), f3, at(hi_)(vreg), ALU.subtract), {})],
                    wide)

        def mixed(s, b, c0, w):
            with TE.If(preg["lo"] < preg["hi"]):
                with TE.Fori(preg["lo"], preg["hi"]) as k:
                    a = AT[:, bass.ds(k, 1), c0:c0 + w].rearrange("p o j -> p (o j)")
                    for part in range(2):
                        TE.matmul(PSALL[:, b, 0:w], den_b[s][:, bass.ds(k, 1), part, :].rearrange("p o j -> p (o j)"),
                                  a, start=False, stop=False)

        num_free = {6: rank_ok["c"], 7: rank_ok["c"]}
        z_free = [zt_free] * 5
        l_free = [m2] * 3
        steps = [(jt, c) for jt in range(T) for c in range(len(CH))]
        leaky_ok, sub_ok, exp_ok, g_ok, ln_ok = {}, {}, {}, {}, {}

        def tz(u):
            return tZ[u % 5][:, 0:CH[steps[u][1]][1]]

        def tl(u):
            return tL[u % 3][:, 0:CH[steps[u][1]][1]]

        def num(u):
            jt, c = steps[u]
            c0, w = CH[c]
            b = 6 + u % 2
            if c == 0:
                pe.wait(win_ok)
                pe.do(window(TE, preg), jt)
            pe.wait(den_ok[jt], num_free[b], tab_ok, E_ok)
            pe.do(TE.matmul, PSALL[:, b, 0:w], EHL[0][:, jt * P:(jt + 1) * P], tab[:, c0:c0 + w],
                  start=True, stop=False)
            pe.do(mixed, (jt + 1) % 2, b, c0, w)
            m = pe.sig(TE.matmul, PSALL[:, b, 0:w], EHL[1][:, jt * P:(jt + 1) * P], tab[:, c0:c0 + w],
                       start=False, stop=True)
            if c == len(CH) - 1:
                den_free[jt] = m
            ac_.wait(m, l_free[u % 3], cst_ok)
            ln_ok[u] = num_free[b] = ac_.sig(S.activation, tl(u), PSALL[:, b, 0:w], ACT.Ln, bias=tiny)

        def scores(u):
            jt, c = steps[u]
            c0, w = CH[c]
            ac_.wait(view_ok["r"], cs_ok, z_free[u % 5])
            z = ac_.sig(S.activation, tz(u), rb[:, c0:c0 + w], ACT.Identity, bias=cs[:, jt:jt + 1])
            dv.wait(z)
            leaky_ok[u] = dv.sig(V.scalar_tensor_tensor, tz(u), tz(u), SLOPE, tz(u), ALU.mult, ALU.max)

        def quotient(u):
            gp.wait(ln_ok[u], leaky_ok[u])
            sub_ok[u] = gp.sig(G.tensor_tensor, tz(u), tz(u), tl(u), ALU.subtract)

        def expo(u):
            ac_.wait(sub_ok[u])
            exp_ok[u] = ac_.sig(S.activation, tz(u), tz(u), ACT.Exp)

        def guard(u):
            dv.wait(exp_ok[u])
            l_free[u % 3] = g_ok[u] = dv.sig(V.scalar_tensor_tensor, tz(u), tl(u), LNZ, tz(u), ALU.is_gt, ALU.mult)

        def ymm(u):
            jt, c = steps[u]
            c0, w = CH[c]
            pe.wait(g_ok[u], XWs_ok)
            z_free[u % 5] = m = pe.sig(TE.matmul, PSALL[:, c, 0:w], XWs[:, jt, :], tz(u),
                                       start=(jt == 0), stop=(jt == T - 1))
            return m

        for stage in range(3):
            den(0, stage)
        scores(0)
        LAG = 3
        n_steps = len(steps)
        for u in range(n_steps + LAG):
            if u < n_steps:
                jt, c = steps[u]
                num(u)
                quotient(u)
            if 0 <= u - 1 < n_steps:
                expo(u - 1)
                guard(u - 1)
            if u >= LAG:
                y_end = ymm(u - LAG)
            if u + 1 < n_steps:
                scores(u + 1)
            if u < n_steps and 1 <= c <= 3 and jt + 1 < T:
                den(jt + 1, c - 1)
        g_ok = g_ok[n_steps - 1]

        YT = R1[:, 0:NP]
        Y3 = R1[:, NP:2 * NP].rearrange("p (t d) -> p t d", t=T)
        Ys = XWs
        xp = R1[:, 2 * NP:3 * NP + NP // 2].bitcast(BF16).rearrange("p (t c d) -> p t c d", t=T, c=3)
        gp.wait(y_end, g_ok)
        yz = gp.sig(G.memset, YT[:, N:NP], 0.0)
        for c, (c0, w) in enumerate(CH):
            ev = ac_ if c % 2 else dv
            ev.wait(y_end, g_ok)
            if c % 2:
                yt_a = ac_.sig(S.activation, YT[:, c0:c0 + w], PSALL[:, c, 0:w], ACT.Copy)
            else:
                yt_d = dv.sig(V.tensor_copy, YT[:, c0:c0 + w], PSALL[:, c, 0:w])
        pe.wait(yt_a, yt_d, yz)
        bfree = {0: yt_a, 1: yt_a}
        for g, (t0, nb) in enumerate(GRP):
            b = g % 2
            pe.wait(bfree[b])
            for q in range(nb):
                m = pe.sig(TE.transpose, PSALL[:, b, q * P:(q + 1) * P], YT[:, (t0 + q) * P:(t0 + q + 1) * P],
                           ident[:, :])
            dv.wait(m)
            bfree[b] = y3_ok = dv.sig(V.tensor_copy, Y3[:, t0:t0 + nb, :],
                                      PSALL[:, b, 0:nb * P].rearrange("p (b d) -> p b d", b=nb))
        sp.wait(y3_ok, y_end)
        sp.dma(s_Yd, nc.sync.dma_start, Yd.rearrange("(t p) d -> p t d", p=P), Y3)
        sp.dma(s_x1b, nc.sync.dma_start, AO3, x1d.rearrange("(t p) d -> p t d", p=P))
        x1b_ok = (s_x1b, 16)
        gp.wait((s_Yd, 16), y_end)
        for t in range(T):
            gp.dma(s_Yg, G.indirect_dma_start, out=Ys[:, t, :], out_offset=None, in_=Yd,
                   in_offset=bass.IndirectOffsetOnAxis(ap=idx[:, 3, t:t + 1], axis=0))
        xp_ok = split3(Ys, xp, None, ((s_Yg, 16 * T), y_end), SL)
        bank_free = [y3_ok] * 8
        outs = {}
        late = None

        def store(item):
            it, mrow, fin = item
            ok = fin()
            sp.wait(ok)
            sp.dma(s_out[it % 2], nc.sync.dma_start, out[it * P:it * P + mrow, :], hb[0:mrow, it % 2, :])
            outs[it] = (s_out[it % 2], 16 * (it // 2 + 1))

        for it in range(T):
            m, mrow, view = spread(it, xp_ok, it % 4, xp)
            s = it % 2
            hh = hb[0:mrow, s, :]
            dv.wait(m, outs.get(it - 2), x1b_ok)
            r = dv.sig(V.tensor_reduce, hh, view, AX.X, ALU.add)
            bank_free[it % 4] = r
            dv.wait(r)
            r = dv.sig(V.tensor_tensor, hh, hh, AO3[0:mrow, it, :], ALU.add)
            _, fin = norm(hh, mrow, it, hh, r)
            if late is not None:
                store(late)
            late = (it, mrow, fin)
        store(late)
        sp.wait(outs[T - 1], outs[T - 2])
        sp.wait(AT_in)

        block = ctx.enter_context(nc.Block())

        @block.sync
        def _(eng):
            sp.emit(eng)

        @block.gpsimd
        def _(eng):
            gp.emit(eng)

        @block.scalar
        def _(eng):
            eng.add_instruction(mybir.InstLoadActFuncSet(act_func_set_id=LN_EXP_SET, engine=mybir.EngineType.Activation,
                                                         name=nc.get_next_instruction_name()))
            ac_.emit(eng)

        @block.vector
        def _(eng):
            dv.emit(eng)

        @block.tensor
        def _(eng):
            pe.emit(eng)


def kernel(x, adj, L0_gnn_t, L0_gnn_alpha, L0_gnn_beta, L1_gnn_W, L1_gnn_a):
    import numpy as np
    import concourse.bacc as bacc
    from concourse.bass_utils import run_bass_kernel_spmd as run

    nc = bacc.Bacc("TRN2", target_bir_lowering=False, num_devices=1)
    x, adj = np.asarray(x), np.asarray(adj)
    xr = np.zeros((NP, D), x.dtype)
    xr[:N] = x
    ar = np.zeros((NP, NP), adj.dtype)
    ar[:N, :N] = adj
    at = np.zeros((NP, N), adj.dtype)
    at[:N] = adj.T
    arrays = {
        "x": xr, "adj": ar, "adjT": at,
        "alpha": np.asarray(L0_gnn_alpha).reshape(1, 1), "beta": np.asarray(L0_gnn_beta).reshape(1, 1),
        "W": np.ascontiguousarray(L1_gnn_W), "a": np.ascontiguousarray(np.asarray(L1_gnn_a).reshape(2, D).T),
    }
    args = [nc.dram_tensor(f"in_{k}", v.shape, mybir.dt.from_np(v.dtype), kind="ExternalInput").ap()
            for k, v in arrays.items()]
    args.append(nc.dram_tensor("out_0", (N, D), F32, kind="ExternalOutput").ap())
    adj_resnorm2_kernel(nc, *args)
    r = run(nc, [{f"in_{k}": v for k, v in arrays.items()}], core_ids=[0])
    return r.results[0]["out_0"]
```

```python
from contextlib import ExitStack

import concourse.bass as bass
from concourse import mybir

P = 128
N = 2708
T = 22
NP = T * P
D = 128
LAST = N - (T - 1) * P
CH = [(c * 452, min(452, N - c * 452)) for c in range(6)]
GRP = [(g * 4, min(4, T - g * 4)) for g in range(6)]
XS = 1024.0
SLOPE = 0.01
R1N = 11286
DEG = 456
EARLY = 11
HB = 5
RW = 452
LN_EXP_SET = 6
WN = 4
TINY = 2.0 ** -64
LNZ = -40.0
WMAX = 80.0
BETA_PLAIN = 16.0
LN_EPS = 1e-5
COS_EPS = 1e-8

ALU = mybir.AluOpType
ACT = mybir.ActivationFunctionType
AX = mybir.AxisListType
F32 = mybir.dt.float32
BF16 = mybir.dt.bfloat16
FP16 = mybir.dt.float16
U32 = mybir.dt.uint32
I32 = mybir.dt.int32


class Line:

    def __init__(self, sem):
        self.sem = sem
        self.n = 0
        self.items = []
        self.met = {}

    def wait(self, *marks):
        for mark in marks:
            if mark is None:
                continue
            sem, v = mark
            if self.met.get(id(sem), 0) < v:
                self.met[id(sem)] = v
                self.items.append(("wait", sem, v, None))

    def do(self, fn, *a, **k):
        self.items.append(("quiet", fn, a, k))

    def sig(self, fn, *a, **k):
        self.n += 1
        self.items.append(("sig", fn, a, k))
        return (self.sem, self.n)

    def dma(self, sem, fn, *a, **k):
        self.items.append(("dma", fn, a, (k, sem)))

    def either(self, flag, small, large):
        self.items.append(("either", flag, (small, large), self.n))
        self.n += len(large)
        return (self.sem, self.n)

    def apart(self, flag, since, n, other):
        mine = self.items[since:]
        del self.items[since:]
        self.items.append(("apart", flag, (mine, other), self.n - n))

    def branch(self, eng, steps, base, total):
        for i, (fn, a, k) in enumerate(steps):
            if i:
                eng.wait_ge(self.sem, base + i)
            fn(*a(), **k).then_inc(self.sem, 1 if i + 1 < len(steps) else total - i)

    def emit(self, eng, items=None):
        for kind, x, a, k in (self.items if items is None else items):
            if kind == "apart":
                with eng.If(x() == 0):
                    self.emit(eng, a[0])
                with eng.Else():
                    line, last = a[1]
                    line.emit(eng)
                    last().then_inc(self.sem, k)
            elif kind == "wait":
                eng.wait_ge(x, a)
            elif kind == "either":
                with eng.If(x() == 0):
                    self.branch(eng, a[0], k, len(a[1]))
                with eng.Else():
                    self.branch(eng, a[1], k, len(a[1]))
            elif kind == "quiet":
                x(*a, **k)
            elif kind == "sig":
                x(*a, **k).then_inc(self.sem, 1)
            else:
                x(*a, **k[0]).then_inc(k[1], 16)


def adj_resnorm2_kernel(nc, x, adjT, alpha, beta, W, a, rowk, out):
    with ExitStack() as ctx:
        def sb(name, shape, dt=F32):
            return ctx.enter_context(nc.sbuf_tensor(name, shape, dt))

        def sem(name):
            return ctx.enter_context(nc.semaphore(name))

        AT = sb("AT", [P, T, N], BF16)
        R1 = sb("R1", [P, R1N])
        X = sb("X", [P, NP])
        AO = sb("AO", [P, NP])
        XN = sb("XN", [P, NP])
        Wt = sb("Wt", [P, D])
        ident = sb("ident", [P, P])
        ac = sb("ac", [P, 2])[:, :]
        sm = sb("sm", [P, 22])
        st = sb("st", [P, 13, T])
        flag = sb("flag", [1, 1], I32)
        ln = sb("ln", [P, 2, 12])
        ring = sb("ring", [P, 6, RW])
        hb = ring[:, 0:HB, 0:D]
        U = sb("U", [P, P], BF16)
        ones = sb("ones", [P, 1], BF16)
        rec = sb("rec", [P, T, 2])
        idx = sb("idx", [P, 4, T], U32)
        mk = sb("mk", [P, T])
        mk2 = ring[:, 5, 256:256 + T]
        kc = sb("kc", [P, 6])
        is_u, is_l, tab_part, e_part, n_above, n_below = (kc[:, q:q + 1] for q in range(6))
        win = sb("win", [1, 4 * T], I32)
        winf = ring[0:1, 5, 0:4 * T]
        racc = {w: ring[:, 4, o:o + 2 * T].rearrange("p (q t) -> p q t", q=2) for w, o in (("r", 0), ("c", 64))}
        tie = ring[:, 3, 0:P].bitcast(BF16).rearrange("p (q j) -> p q j", q=2)

        PSALL = ctx.enter_context(nc.psum_tensor("PSALL", [P, 8, 512], F32))

        X3 = X[:, :].rearrange("p (t d) -> p t d", t=T)
        AO3 = AO[:, :].rearrange("p (t d) -> p t d", t=T)
        xh = AO[:, 0:NP // 2].bitcast(BF16).rearrange("p (t d) -> p t d", t=T)
        xl = AO[:, NP // 2:NP].bitcast(BF16).rearrange("p (t d) -> p t d", t=T)
        Mb = R1[:, 0:NP]
        AOT = R1[:, NP:2 * NP]
        ES = R1[:, 2 * NP:3 * NP]
        Fp = [R1[:, 3 * NP + q * RW:3 * NP + (q + 1) * RW].bitcast(BF16) for q in range(6)]
        xnh = XN[:, 0:NP // 2].bitcast(FP16)
        xnl = XN[:, NP // 2:NP].bitcast(FP16)
        xp = R1[:, 3 * NP:4 * NP].bitcast(FP16).rearrange("p (t c d) -> p t c d", t=T, c=2)
        XWs = XN[:, :].rearrange("p (t d) -> p t d", t=T)
        srows = XN[0:2, :]
        rb = R1[:, 0:NP]
        cb = X[:, :]
        XWn = R1[:, NP:NP + T * (D + 1)].rearrange("p (t d) -> p t d", t=T)
        x1T = [R1[:, q * 512:(q + 1) * 512] for q in range(2)]
        XWT = [R1[:, 1024 + q * 512:1024 + (q + 1) * 512] for q in range(2)]
        Cb = [R1[:, 5654 + q * 1408:5654 + (q + 1) * 1408].bitcast(BF16) for q in range(4)]
        W3 = [XN[:, q * 1408:(q + 1) * 1408].bitcast(BF16) for q in range(2)]
        zt = R1[:, 2 * NP:3 * NP]
        den_f = [R1[:, NP:2 * NP], R1[:, 2 * NP:3 * NP]]
        den_b = [v.bitcast(BF16).rearrange("p (t c j) -> p t c j", t=T, c=2) for v in den_f]
        fw = R1[:, 3 * NP:3 * NP + WN * P]
        tab = R1[:, 3 * NP + WN * P:3 * NP + WN * P + N // 2].bitcast(BF16)
        Ehi, EX = (AO[:, q * 1408:(q + 1) * 1408].bitcast(BF16) for q in range(2))
        rest = 3 * NP + WN * P + N // 2
        spare = [AO[:, q * RW:(q + 1) * RW] for q in range(3)]
        slots = [ring[:, q, :] for q in range(6)] + [R1[:, rest + q * RW:rest + (q + 1) * RW] for q in range(2)] + spare
        NZ, NL = 7, 4
        tL, tZ = slots[3:3 + NL], slots[0:3] + slots[3 + NL:]
        bcol, sig, eal, mone = sm[:, 0:1], sm[:, 1:2], sm[:, 2:3], sm[:, 3:4]
        braw, araw = sm[:, 4:5], sm[:, 5:6]
        half, mhalf = sm[:, 7:8], sm[:, 8:9]
        tiny, ref, is0 = sm[:, 9:10], sm[:, 10:11], sm[:, 11:12]
        onec, colsum = sm[:, 15:16], is0
        pm, top = sm[:, 16:17], sm[0:1, 17:18]
        up_x, down_x, up_y, down_y = (sm[:, q:q + 1] for q in range(18, 22))
        sq, nrm, rn, deg, dis, rs, rrs, scol, srow, cs, rsrt, wu, wl = (st[:, i, :] for i in range(13))

        s_pe, s_dv, s_ac, s_gp = sem("s_pe"), sem("s_dv"), sem("s_ac"), sem("s_gp")
        s_x, s_w, s_const = sem("s_x"), sem("s_w"), sem("s_const")
        s_AT = [sem(f"s_AT{i}") for i in range(T)]
        s_ATd, s_x1, s_sd, s_sb, s_sc, s_sr, s_rt, s_ct, s_cr, s_Yd = (
            sem(n) for n in ("s_ATd", "s_x1", "s_sd", "s_sb", "s_sc", "s_sr", "s_rt", "s_ct", "s_cr", "s_Yd"))
        s_Yg = [sem(f"s_Yg{i}") for i in range(4)]
        s_x1b, s_xw = sem("s_x1b"), sem("s_xw")
        s_out = [sem(f"s_out{i}") for i in range(HB)]

        ATd = nc.dram_tensor("ATd", (NP, N), BF16, kind="Internal").ap()
        x1d = nc.dram_tensor("x1d", (NP, D), F32, kind="Internal").ap()
        sd = nc.dram_tensor("sd", (2, NP), F32, kind="Internal").ap()
        XWd = nc.dram_tensor("XWd", (NP, D + 1), F32, kind="Internal").ap()
        RKd = nc.dram_tensor("RKd", (NP, 2), F32, kind="Internal").ap()
        Yd = nc.dram_tensor("Yd", (NP, D), F32, kind="Internal").ap()

        pe, dv, ac_, gp, sp = Line(s_pe), Line(s_dv), Line(s_ac), Line(s_gp), Line(None)
        V, S, G, TE = nc.vector, nc.scalar, nc.gpsimd, nc.tensor

        sp.dma(s_x, nc.sync.dma_start, X3, x.rearrange("(t p) d -> p t d", p=P))
        x_in = (s_x, 16)
        small = [(Wt[:, :], W), (ac, a), (kc[:, :], rowk),
                 (braw, beta.broadcast_to([P, 1])), (araw, alpha.broadcast_to([P, 1]))]
        for dst, src in small:
            sp.dma(s_w, nc.sync.dma_start, dst, src)
        w_in = (s_w, 16 * len(small))

        m = gp.sig(G.memset, ident[:, :], 0.0)
        gp.wait(m)
        id_ok = gp.sig(G.affine_select, out=ident[:, :], in_=ident[:, :], compare_op=ALU.not_equal, fill=1.0,
                       base=0, pattern=[[-1, P]], channel_multiplier=1)
        gp.sig(G.memset, half, 0.5)
        pc_ok = gp.sig(G.memset, mhalf, -0.5)
        gp.sig(G.memset, tiny, TINY)
        gp.sig(G.memset, ones[:, :], 1.0)
        gp.sig(G.memset, sm[:, 3:4], -1.0)
        gp.sig(G.memset, sm[:, 15:16], 1.0)
        gp.sig(G.memset, U[:, :], 1.0)
        m = gp.sig(G.iota, idx[:, 0, :].bitcast(I32), pattern=[[P, T]], base=0, channel_multiplier=1)
        gp.wait(m)
        gp.sig(G.affine_select, out=U[:, :], in_=U[:, :], compare_op=ALU.is_gt, fill=0.0,
               base=0, pattern=[[-1, P]], channel_multiplier=1)
        gp.sig(G.iota, idx[:, 3, :].bitcast(I32), pattern=[[P, T]], base=0, channel_multiplier=0)
        gp.wait((s_gp, gp.n))
        row_ok = gp.sig(G.memset, ring[0:1, 5, 0:P], 1.0)
        cst_ok = row_ok
        gp.wait(cst_ok)

        def load_AT(kt, gp=gp):
            gp.dma(s_AT[kt], G.dma_start, AT[:, kt, :], adjT[kt * P:(kt + 1) * P, :])

        AT_in = [(s_AT[kt], 16) for kt in range(T)]
        for kt in range(4):
            load_AT(kt)

        xx = AO3
        halves = ((0, 11), (11, 11))
        for t0, nt in halves:
            ac_.wait(x_in)
            m = ac_.sig(S.activation, xx[:, t0:t0 + nt, :], X3[:, t0:t0 + nt, :], ACT.Square)
            dv.wait(m)
            m = dv.sig(V.tensor_reduce, sq[:, t0:t0 + nt], xx[:, t0:t0 + nt, :], AX.X, ALU.add)
        pe.wait(cst_ok, x_in)
        for t in range(T):
            cm = pe.sig(TE.matmul, PSALL[:, 4, 0:1], X3[:, t, :], onec, start=(t == 0), stop=(t == T - 1))
        ac_.wait(cm)
        cs_ready = ac_.sig(S.activation, colsum, PSALL[:, 4, 0:1], ACT.Copy)
        gp.wait(m, pc_ok)
        m = gp.sig(G.tensor_tensor, nrm, sq, half.broadcast_to([P, T]), ALU.pow)
        for kt in range(4, EARLY):
            load_AT(kt)
        dv.wait(m)
        m = dv.sig(V.tensor_scalar, nrm, nrm, COS_EPS, 1.0 / XS, ALU.max, ALU.mult)
        dv.wait(m)
        m = dv.sig(V.reciprocal, rn, nrm)
        dv.wait(m)
        free = [None, None]
        split = None
        halves_ready = []

        def fp16_parts(b, c0, w, ready):
            nonlocal split
            ac_.wait(ready)
            h = ac_.sig(S.activation, xnh[:, c0:c0 + w], PSALL[:, b, 0:w], ACT.Copy)
            dv.wait(h)
            split = free[b] = dv.sig(V.tensor_tensor, xnl[:, c0:c0 + w], PSALL[:, b, 0:w], xnh[:, c0:c0 + w],
                                     ALU.subtract)

        for g, (t0, nb) in enumerate(GRP):
            b = g % 2
            dv.wait(m)
            xn_ok = dv.sig(V.tensor_tensor, AO3[:, t0:t0 + nb, :], X3[:, t0:t0 + nb, :],
                           rn[:, t0:t0 + nb].unsqueeze(2).broadcast_to([P, nb, D]), ALU.mult)
            pe.wait(xn_ok, id_ok, free[b])
            for q in range(nb):
                mt = pe.sig(TE.transpose, PSALL[:, b, q * P:(q + 1) * P], AO3[:, t0 + q, :], ident[:, :])
            halves_ready.append((b, t0 * P, nb * P, mt))
            if g:
                fp16_parts(*halves_ready[g - 1])
        fp16_parts(*halves_ready[-1])
        m = mt
        ac_.wait(m)
        h = ac_.sig(S.activation, xh, X3, ACT.Copy)
        gp.wait(h)
        x_rest = gp.sig(G.tensor_tensor, xl[:, 4:T, :], X3[:, 4:T, :], xh[:, 4:T, :], ALU.subtract)
        dv.wait(h)
        x_first = dv.sig(V.tensor_tensor, xl[:, 0:4, :], X3[:, 0:4, :], xh[:, 0:4, :], ALU.subtract)

        def scale_of(ok, bank, orow, orow_ok, factor, up, down):
            pe.wait(ok, id_ok)
            m = pe.sig(TE.transpose, PSALL[0:1, bank, 0:P], pm, ident[:, :])
            dv.wait(m)
            m = dv.sig(V.tensor_reduce, top, PSALL[0:1, bank, 0:P], AX.X, ALU.max)
            dv.wait(m)
            m = dv.sig(V.tensor_scalar, top, top, 1e-30, None, ALU.max)
            pe.wait(m, orow_ok)
            m = pe.sig(TE.matmul, PSALL[:, bank, 0:1], orow, top, start=True, stop=True)
            dv.wait(m)
            m = dv.sig(V.tensor_scalar, down, PSALL[:, bank, 0:1], factor * 2.0 ** -14, None, ALU.mult)
            dv.wait(m)
            return dv.sig(V.reciprocal, up, down)

        m = dv.sig(V.tensor_reduce, pm, nrm, AX.X, ALU.max)
        up_ok = scale_of(m, 5, ring[0:1, 5, 0:P], row_ok, XS, up_x, down_x)
        ac_.wait(w_in)
        e = ac_.sig(S.activation, eal, araw, ACT.Exp, scale=-1.0)
        dv.wait(e)
        m = dv.sig(V.tensor_scalar, eal, eal, 1.0, None, ALU.add)
        dv.wait(m)
        sig_ok = dv.sig(V.reciprocal, sig, eal)
        dv.wait(w_in, sig_ok)
        bc_ok = dv.sig(V.tensor_scalar, bcol, braw, 1.0 / (XS * XS), None, ALU.mult)
        m = dv.sig(V.tensor_tensor, eal[0:1, :], braw[0:1, :], braw[0:1, :], ALU.mult)
        dv.wait(m)
        m = dv.sig(V.tensor_scalar, eal[0:1, :], eal[0:1, :], BETA_PLAIN ** 2, None, ALU.is_gt)
        dv.wait(m)
        flag_ok = dv.sig(V.tensor_copy, flag[:, :], eal[0:1, :])

        def attention(pe, dv, ac_, gp, shifted):
            zf, ff, bf = [None] * 6, [None] * 6, {6: None, 7: None}
            u = 0
            unit = [(jt, c) for jt in range(T) for c in range(len(CH))]

            def logits(jt, c, b):
                rows = P if jt < T - 1 else LAST
                c0, w = CH[c]
                pe.wait(split, bf[b])
                for k, (lh, rh) in enumerate(((xnh, xnh), (xnh, xnl), (xnl, xnh))):
                    args = (PSALL[0:rows, b, 0:w], lh[:, jt * P:jt * P + rows], rh[:, c0:c0 + w])
                    m = (pe.sig if k == 2 else pe.do)(TE.matmul, *args, start=(k == 0), stop=(k == 2))
                return m, rows, c0, w

            if shifted:
                for kt in range(EARLY, T):
                    load_AT(kt, gp)
                for u, (jt, c) in enumerate(unit):
                    b = 6 + u % 2
                    m, rows, c0, w = logits(jt, c, b)
                    z = ring[0:rows, u % 6, 0:w]
                    M = Mb[0:rows, c0:c0 + w]
                    dv.wait(m, AT_in[jt], bc_ok, zf[u % 6])
                    bf[b] = m = dv.sig(V.scalar_tensor_tensor, z, PSALL[0:rows, b, 0:w], bcol[0:rows, :],
                                       AT[0:rows, jt, c0:c0 + w], ALU.mult, ALU.mult)
                    dv.wait(m)
                    zf[u % 6] = m = dv.sig(V.tensor_copy, M, z) if jt == 0 else \
                        dv.sig(V.tensor_tensor, M, M, z, ALU.max)
                    dv.wait(m)
                o, dg = R1[:, NP:NP + P], R1[:, NP + P:NP + 2 * P]
                o_ok = gp.sig(G.memset, o, 1.0)
                for t in range(T):
                    cols = P if t < T - 1 else LAST
                    M = Mb[:, t * P:t * P + cols]
                    pe.wait(m, id_ok, o_ok)
                    m = pe.sig(TE.transpose, PSALL[0:cols, 6, 0:P], M, ident[:, :])
                    dv.wait(m, id_ok)
                    m = dv.sig(V.tensor_reduce, eal[0:cols, :], PSALL[0:cols, 6, 0:P], AX.X, ALU.max)
                    dv.wait(m)
                    m = dv.sig(V.tensor_scalar, dg[0:cols, :], ident[0:cols, :], eal[0:cols, :], None, ALU.mult)
                    pe.wait(m)
                    m = pe.sig(TE.matmul, PSALL[:, 7, 0:cols], o[0:cols, :], dg[0:cols, 0:cols], start=True, stop=True)
                    dv.wait(m)
                    m = dv.sig(V.tensor_copy, M, PSALL[:, 7, 0:cols])
                ff = [m] * 6
                bf = {6: m, 7: m}
            e_ok, f_ok, s_ok = {}, {}, {}
            es_free = None
            dg = [dv.sig(V.memset, deg, 0.0)]
            dis_at = []

            def expo(u):
                nonlocal es_free
                jt, c = unit[u]
                b = 6 + u % 2
                m, rows, c0, w = logits(jt, c, b)
                z = ring[0:rows, u % 6, 0:w]
                a = AT[0:rows, jt, c0:c0 + w]
                if c == 0:
                    pe.wait(AT_in[jt], cst_ok)
                    for t in range(T):
                        c1 = min(t * P + P, N)
                        m = pe.sig(TE.matmul, PSALL[0:c1 - t * P, b, DEG + t:DEG + t + 1],
                                   AT[0:rows, jt, t * P:c1], ones[0:rows, :], start=True, stop=True)
                dv.wait(m, AT_in[jt], bc_ok, zf[u % 6], s_ok.get(u - 6))
                if c == 0:
                    dv.wait(*dg)
                    dg[:] = [dv.sig(V.tensor_tensor, deg[0:e1, a:z], deg[0:e1, a:z], PSALL[0:e1, b, DEG + a:DEG + z],
                                    ALU.add) for e1, a, z in ((P, 0, T - 1), (LAST, T - 1, T))]
                    if jt == T - 1:
                        dv.wait(*dg)
                        d = dv.sig(V.tensor_scalar, dis, deg, 1.0, None, ALU.max)
                        gp.wait(d, pc_ok)
                        dis_at.append(gp.sig(G.tensor_tensor, dis, dis, mhalf.broadcast_to([P, T]), ALU.pow))
                if shifted:
                    bf[b] = m = dv.sig(V.scalar_tensor_tensor, z, PSALL[0:rows, b, 0:w], bcol[0:rows, :], a,
                                       ALU.mult, ALU.mult)
                    dv.wait(m)
                    m = dv.sig(V.tensor_tensor, z, z, Mb[0:rows, c0:c0 + w], ALU.subtract)
                    ac_.wait(m)
                    e = ac_.sig(S.activation, z, z, ACT.Exp)
                else:
                    bf[b] = m = dv.sig(V.tensor_tensor, z, PSALL[0:rows, b, 0:w], a, ALU.mult)
                    ac_.wait(m, bc_ok)
                    e = ac_.sig(S.activation, z, z, ACT.Exp, scale=bcol[0:rows, :])
                ac_.wait(e, ff[u % 6])
                fh = Fp[u % 6][0:rows, 0:w]
                if shifted:
                    h = ac_.sig(S.activation, fh, z, ACT.Copy)
                else:
                    ac_.wait(cst_ok)
                    h = ac_.sig(S.activation, fh, z, ACT.Identity, bias=mone[0:rows, :])
                e_ok[u] = h
                gp.wait(e)
                S_ = ES[0:rows, c0:c0 + w]
                s_ok[u] = gp.sig(G.tensor_copy, S_, z) if jt == 0 else gp.sig(G.tensor_tensor, S_, S_, z, ALU.add)

            def low(u):
                jt, c = unit[u]
                rows, w = (P if jt < T - 1 else LAST), CH[c][1]
                z, F = ring[0:rows, u % 6, 0:w], Fp[u % 6]
                dv.wait(e_ok[u])
                if shifted:
                    f = dv.sig(V.tensor_tensor, F[0:rows, RW:RW + w], z, F[0:rows, 0:w], ALU.subtract)
                else:
                    f = dv.sig(V.scalar_tensor_tensor, F[0:rows, RW:RW + w], z, 1.0, F[0:rows, 0:w],
                               ALU.subtract, ALU.subtract)
                f_ok[u] = zf[u % 6] = f

            def gather(u):
                jt, c = unit[u]
                rows, w = (P if jt < T - 1 else LAST), CH[c][1]
                F = Fp[u % 6]
                pe.wait(f_ok[u], x_first if jt < 4 else x_rest, up_ok, cs_ready)
                for k, (xx, o) in enumerate(((xh, 0), (xl, 0), (xh, RW))):
                    m = (pe.sig if k == 2 else pe.do)(TE.matmul, PSALL[:, c, 0:w], xx[0:rows, jt, :],
                                                      F[0:rows, o:o + w], start=(jt == 0 and k == 0),
                                                      stop=(jt == T - 1 and k == 2))
                ff[u % 6] = m
                return m

            n = len(unit)
            for u in range(n + 4):
                if u < n:
                    expo(u)
                if 0 <= u - 2 < n:
                    low(u - 2)
                if u >= 4:
                    m = gather(u - 4)
                if not shifted and u % 6 == 5 and EARLY + u // 6 < T:
                    load_AT(EARLY + u // 6, gp)
            for c, (c0, w) in enumerate(CH):
                ev = dv if c % 2 else ac_
                ev.wait(m, cs_ready)
                dst, src = AOT[:, c0:c0 + w], PSALL[:, c, 0:w]
                if c % 2 and shifted:
                    t_d = dv.sig(V.tensor_copy, dst, src)
                elif c % 2:
                    t_d = dv.sig(V.tensor_scalar, dst, src, colsum, None, ALU.add)
                elif shifted:
                    t_a = ac_.sig(S.activation, dst, src, ACT.Copy)
                else:
                    t_a = ac_.sig(S.activation, dst, src, ACT.Identity, bias=colsum)
            return dis_at[0]

        def beta_flag(e, reg):
            def load():
                reg["beta"] = e.value_load(flag[0:1, 0:1], min_val=0, max_val=1)
            return load

        main_lines, engines = (pe, dv, ac_, gp), (TE, V, S, G)
        regs = ({}, {}, {}, {})
        marks = []
        for line, e, reg in zip(main_lines, engines, regs):
            line.wait(flag_ok)
            line.do(beta_flag(e, reg))
            marks.append((len(line.items), line.n))
        other = tuple(Line(sem(f"s_{q}2")) for q in ("pe", "dv", "ac", "gp"))
        attention(*other, True)
        ends = [(o.sem, o.n) for o in other]
        for o in other:
            o.wait(*ends)
        dis_ok = attention(*main_lines, False)
        last_steps = (lambda: TE.matmul(PSALL[0:1, 6, 0:1], onec, onec, start=True, stop=True),
                      lambda: V.memset(eal[:, :], 0.0),
                      lambda: S.activation(st[:, 6, 0:1], ident[:, 0:1], ACT.Copy),
                      lambda: G.memset(st[:, 6, 1:2], 0.0))
        for line, reg, (since, n), o, last in zip(main_lines, regs, marks, other, last_steps):
            line.apart((lambda reg: lambda: reg["beta"])(reg), since, n, (o, last))
        all_free = [(line.sem, line.n) for line in main_lines]

        sp.wait(*AT_in)
        for q in range(2):
            sp.dma(s_ATd, nc.sync.dma_start, ATd[q * 11 * P:(q + 1) * 11 * P, :].rearrange("(t p) n -> p t n", p=P),
                   AT[:, q * 11:(q + 1) * 11, :])

        def split2(src3, dst, up, first, slices):
            done = []
            for k, (t0, nt) in enumerate(slices):
                sl = src3[:, t0:t0 + nt, :]
                dv.wait(*(first[k] if isinstance(first, list) else first))
                h = dv.sig(V.tensor_scalar, dst[:, t0:t0 + nt, 0, :], sl, up, None, ALU.mult)
                dv.wait(h)
                done.append(dv.sig(V.scalar_tensor_tensor, dst[:, t0:t0 + nt, 1, :], sl, up, dst[:, t0:t0 + nt, 0, :],
                                   ALU.mult, ALU.subtract))
            return done

        SL = [(0, 6), (6, 6), (12, 6), (18, 4)]
        xd3 = R1[:, 0:NP].rearrange("p (t d) -> p t d", t=T)
        z_ok = gp.sig(G.memset, AOT[:, N:NP], 0.0)
        pe.wait(*all_free)
        dv.wait(*all_free)
        dv.wait(dis_ok, up_ok)
        xp_ok = []
        for t0, nt in SL:
            m = dv.sig(V.tensor_tensor, xd3[:, t0:t0 + nt, :], X3[:, t0:t0 + nt, :],
                       dis[:, t0:t0 + nt].unsqueeze(2).broadcast_to([P, nt, D]), ALU.mult)
            xp_ok += split2(xd3, xp, up_x, (m,), [(t0, nt)])
        down_ok = dv.sig(V.tensor_scalar, rn, dis, down_x, None, ALU.mult)
        ao_ok = {}
        xw_free = {4: None, 5: None, 6: None, 7: None}

        def row_sums():
            for t in range(T):
                rows = P if t < T - 1 else LAST
                m = pe.sig(TE.matmul, PSALL[0:rows, 5, t:t + 1], ES[:, t * P:t * P + rows], onec,
                           start=True, stop=True)
            z1 = dv.sig(V.memset, rs, 1.0)
            dv.wait(m, z1)
            rd = [dv.sig(V.tensor_copy, rs[:, 0:T - 1], PSALL[:, 5, 0:T - 1]),
                  dv.sig(V.tensor_copy, rs[0:LAST, T - 1:T], PSALL[0:LAST, 5, T - 1:T])]
            xw_free[5] = rd[1]
            dv.wait(*rd)
            return dv.sig(V.reciprocal, rrs, rs)

        def attn_rows(g, rs_ok):
            t0, nb = GRP[g]
            b = 6 + g % 2
            pe.wait(xw_free[b], z_ok)
            for q in range(nb):
                m = pe.sig(TE.transpose, PSALL[:, b, q * P:(q + 1) * P], AOT[:, (t0 + q) * P:(t0 + q + 1) * P],
                           ident[:, :])
            sl = AO3[:, t0:t0 + nb, :]
            dv.wait(m, rs_ok)
            xw_free[b] = m = dv.sig(V.tensor_tensor, sl, PSALL[:, b, 0:nb * P].rearrange("p (b d) -> p b d", b=nb),
                                    rrs[:, t0:t0 + nb].unsqueeze(2).broadcast_to([P, nb, D]), ALU.mult)
            dv.wait(m)
            ao_ok[g] = dv.sig(V.tensor_tensor, sl, sl, X3[:, t0:t0 + nb, :], ALU.subtract)

        bank_free = [None] * 8
        hb_free = [None, None]
        x1_ok = {}

        def spread(it, parts_ok, bank, xp):
            mrow = P if it < T - 1 else LAST
            pe.wait(bank_free[bank])
            for jt in range(T):
                for (t0, nt), ok in zip(SL, parts_ok):
                    if jt == t0:
                        pe.wait(ok)
                args = (PSALL[0:mrow, bank, 0:2 * D], AT[:, jt, it * P:it * P + mrow],
                        xp[:, jt, :, :].rearrange("p c d -> p (c d)"))
                kw = dict(start=(jt == 0), stop=(jt == T - 1))
                if jt == T - 1:
                    m = pe.sig(TE.matmul, *args, **kw)
                else:
                    pe.do(TE.matmul, *args, **kw)
            return m, mrow, PSALL[0:mrow, bank, 0:2 * D].rearrange("p (c d) -> p d c", c=2)

        def norm(h, mrow, it, dst, ok):
            s = it % 2
            dv.wait(ok)
            b = dv.sig(V.bn_stats, ln[0:mrow, s, 0:6], h)
            dv.wait(b)
            b = dv.sig(V.bn_aggr, ln[0:mrow, s, 6:8], ln[0:mrow, s, 0:6])
            dv.wait(b)
            b = dv.sig(V.tensor_scalar, ln[0:mrow, s, 8:9], ln[0:mrow, s, 7:8], LN_EPS, None, ALU.add)
            gp.wait(b)
            b = gp.sig(G.tensor_tensor, ln[0:mrow, s, 9:10], ln[0:mrow, s, 8:9], mhalf[0:mrow, :], ALU.pow)
            return b, (lambda: (dv.wait(b), dv.sig(V.tensor_scalar, dst, h, ln[0:mrow, s, 6:7],
                                                   ln[0:mrow, s, 9:10], ALU.subtract, ALU.mult))[1])

        pe.wait(*AT_in)
        late = None
        gp.wait(*all_free)
        gz = gp.sig(G.memset, hb[:, 0:2, :], 0.0)

        def layer0_tail(it, m, mrow, view):
            s = it % 2
            hh = hb[0:mrow, s, :]
            dv.wait(m, hb_free[s], sig_ok, gz, ao_ok[it // 4], down_ok)
            r = dv.sig(V.tensor_reduce, hh, view, AX.X, ALU.add)
            bank_free[it % 4] = r
            dv.wait(r)
            r = dv.sig(V.scalar_tensor_tensor, hh, hh, rn[0:mrow, it:it + 1], X3[0:mrow, it, :],
                       ALU.mult, ALU.subtract)
            dv.wait(r)
            r = dv.sig(V.scalar_tensor_tensor, hh, AO3[0:mrow, it, :], sig[0:mrow, :], hh, ALU.mult, ALU.add)
            dv.wait(r)
            r = dv.sig(V.tensor_tensor, hh, hh, X3[0:mrow, it, :], ALU.add)
            return norm(hh, mrow, it, AO3[0:mrow, it, :], r)

        def flush(item):
            it, fin = item
            if it == T - 1:
                z = dv.sig(V.memset, AO3[:, it, :], 0.0)
                dv.wait(z)
            x1_ok[it] = hb_free[it % 2] = fin()

        xw = {}
        xw_end = xwn_ok = srow_ok = None

        def xw_rows(g):
            t0, nb = GRP[g]
            w = nb * P
            pe.wait(x1_ok[t0 + nb - 1], xw_free[4])
            for q in range(nb):
                m = pe.sig(TE.transpose, PSALL[:, 4, q * P:(q + 1) * P], AO3[:, t0 + q, :], ident[:, :])
            ac_.wait(m, xw.get(("used", g - 2)))
            xw["x1T", g] = xw_free[4] = ac_.sig(S.activation, x1T[g % 2][:, 0:w], PSALL[:, 4, 0:w], ACT.Copy)

        def xw_products(g):
            nonlocal xwn_ok
            t0, nb = GRP[g]
            w = nb * P
            pe.wait(xw["x1T", g], w_in, xw_free[5])
            m = pe.sig(TE.matmul, PSALL[:, 5, 0:w], Wt[:, :], x1T[g % 2][:, 0:w], start=True, stop=True)
            ac_.wait(m)
            xw["XWT", g] = xw_free[5] = ac_.sig(S.activation, XWT[g % 2][:, 0:w], PSALL[:, 5, 0:w], ACT.Copy)
            pe.wait(xw_free[6])
            for q in range(nb):
                m = pe.sig(TE.matmul, PSALL[:, 6, q * P:(q + 1) * P], x1T[g % 2][:, q * P:(q + 1) * P], Wt[:, :],
                           start=True, stop=True)
            ac_.wait(m)
            xwn_ok = xw_free[6] = ac_.sig(S.activation, XWn[:, t0:t0 + nb, 0:D],
                                          PSALL[:, 6, 0:w].rearrange("p (b d) -> p b d", b=nb), ACT.Copy)

        def xw_scores(g):
            nonlocal srow_ok, xw_end
            t0, nb = GRP[g]
            w = nb * P
            pe.wait(xw["XWT", g], xw_free[7])
            xw_end = xw["used", g] = m = pe.sig(TE.matmul, PSALL[0:2, 7, 0:w], ac, XWT[g % 2][:, 0:w],
                                                start=True, stop=True)
            ac_.wait(m)
            srow_ok = xw_free[7] = ac_.sig(S.activation, srows[:, t0 * P:t0 * P + w], PSALL[0:2, 7, 0:w], ACT.Copy)

        behind = {}
        for g, (t0, nb) in enumerate(GRP):
            for k, part in enumerate((xw_rows, xw_products, xw_scores)):
                behind.setdefault(min(t0 + nb + 1 + k, T), []).append((part, g))

        rs_ok = row_sums()
        for it in range(T):
            m, mrow, view = spread(it, xp_ok, it % 4, xp)
            if it < len(GRP):
                attn_rows(it, rs_ok)
            for part, g in behind.get(it, []):
                part(g)
            if it == T - 1:
                flush(late)
                late = None
            _, fin = layer0_tail(it, m, mrow, view)
            if late is not None:
                flush(late)
            late = (it, fin)
        p2_end = m
        flush(late)
        for part, g in behind[T]:
            part(g)
        bfree = dict((b, x1_ok[T - 1]) for b in range(4))
        bfree.update(xw_free)

        sp.wait(srow_ok, xw_end)
        sp.dma(s_sd, nc.sync.dma_start, sd, srows)
        sd_ok = (s_sd, 16)
        sp.wait(sd_ok, xwn_ok)
        ac_.wait(sd_ok)
        sp.dma(s_sb, nc.sync.dma_start, rb, sd[1:2, :].broadcast_to([P, NP]))
        sp.dma(s_sc, nc.sync.dma_start, cb, sd[0:1, :].broadcast_to([P, NP]))
        sp.wait(x1_ok[T - 1])
        sp.dma(s_x1, nc.sync.dma_start, x1d.rearrange("(t p) d -> p t d", p=P), AO3)
        ac_.dma(s_sb, nc.scalar.dma_start, srow.unsqueeze(2), sd[1:2, :].rearrange("o (t p u) -> (o p) t u", p=P, u=1),
                allow_slow_non_contiguous=True)
        ac_.dma(s_sc, nc.scalar.dma_start, scol.unsqueeze(2), sd[0:1, :].rearrange("o (t p u) -> (o p) t u", p=P, u=1),
                allow_slow_non_contiguous=True)
        view_ok = {"r": (s_sb, 32), "c": (s_sc, 32)}

        MID, REFS = 13, 5
        onesf, rs4, selr = (ring[:, q, 0:P] for q in range(3))
        gp.wait(x1_ok[T - 1])
        gp.sig(G.memset, onesf, 1.0)
        gp.sig(G.memset, rs4, 0.0)
        e = gp.sig(G.memset, selr, 0.0)
        gp.wait(e)
        sel_ok = gp.sig(G.memset, selr[0:1, :], 1.0)
        gp.wait(sel_ok, sd_ok, srow_ok)
        w3_zero = gp.sig(G.memset, XN[:, :], 0.0)
        gp.wait(w3_zero)
        c_free = [(xw_end,)] * 3
        a_ok = None
        cn = 0
        base = sq
        base_ok = dv.sig(V.tensor_copy, base, idx[:, 3, :])
        PARTS = {"r": [(0, 6, 0), (6, 6, 1), (12, 6, 2), (18, 4, 3)], "c": [(0, 7, 5), (7, 7, 6), (14, 8, 7)]}
        VIEW = {"r": (rb, srow, 1), "c": (cb, scol, 2)}
        settled = {}
        marks = {}

        def rank_start(which):
            acc = racc[which]
            dv.wait(view_ok[which], cst_ok, *bfree.values())
            z = [dv.sig(V.memset, acc, 0.0)]
            for t0, nt, bank in PARTS[which]:
                z.append(dv.sig(V.memset, PSALL[:, bank, 0:T * nt], 0.0))
            dv.wait(z[0])
            pe.wait(*z, cst_ok)
            marks[which] = z[0]

        def rank_step(which, lt):
            nonlocal cn, a_ok
            bc, per, _ = VIEW[which]
            acc = racc[which]
            q = cn % 3
            cn += 1
            lo, hi = lt * P, (lt + 1) * P
            end = min(hi, N)
            rows = end - lo
            sc1 = per[0:rows, lt:lt + 1]
            C = Cb[q][0:rows, :]
            t2 = tie[0:rows, cn % 2, 0:rows]
            dv.wait(*c_free[q])
            e = dv.sig(V.scalar_tensor_tensor, t2, bc[0:rows, lo:end], sc1, U[0:rows, 0:rows], ALU.is_equal, ALU.mult)
            if hi < N:
                c_ok = dv.sig(V.tensor_scalar, C[:, hi:N], bc[0:rows, hi:N], sc1, None, ALU.is_lt)
                ac_.wait(c_ok, marks[which], xw_end, a_ok)
                a_ok = ac_.sig(S.activation, Cb[3][0:rows, hi:N], C[:, hi:N], ACT.Copy,
                               accum_out=acc[0:rows, 0, lt:lt + 1])
                pe.wait(c_ok)
                for t0, nt, bank in PARTS[which]:
                    for t in range(max(t0, lt + 1), t0 + nt):
                        c1 = min(t * P + P, N)
                        col = lt * nt + t - t0
                        m = pe.sig(TE.matmul, PSALL[0:c1 - t * P, bank, col:col + 1], C[:, t * P:c1],
                                   ones[0:rows, :], start=True, stop=True)
            dv.wait(e)
            d_ok = dv.sig(V.scalar_tensor_tensor, C[:, lo:end], bc[0:rows, lo:end], sc1, t2, ALU.is_lt, ALU.add,
                          accum_out=acc[0:rows, 1, lt:lt + 1])
            if hi < N:
                c_free[q] = (m, a_ok, d_ok)
                marks[which, lt] = (m, a_ok, d_ok)
            else:
                marks[which, lt] = (d_ok,)

        def settle(which, g):
            t0, nt, bank = PARTS[which][g]
            slot = VIEW[which][2]
            acc = racc[which]
            last = t0 + nt - 1
            sl = slice(t0, t0 + nt)
            dv.wait(*marks[which, last], *marks[which, max(0, last - 1)], base_ok)
            m = dv.sig(V.tensor_tensor, acc[:, 0, sl], acc[:, 0, sl], acc[:, 1, sl], ALU.add)
            dv.wait(m)
            z = dv.sig(V.tensor_reduce, acc[:, 1, sl], PSALL[:, bank, 0:T * nt].rearrange("p (l t) -> p t l", l=T),
                       AX.X, ALU.add)
            dv.wait(z)
            m = dv.sig(V.tensor_tensor, acc[:, 0, sl], acc[:, 0, sl], acc[:, 1, sl], ALU.subtract)
            dv.wait(m)
            m = dv.sig(V.tensor_tensor, acc[:, 0, sl], acc[:, 0, sl], base[:, sl], ALU.add)
            if last < T - 1:
                dv.wait(m)
                settled[which, g] = dv.sig(V.tensor_copy, idx[:, slot, sl], acc[:, 0, sl])
            else:
                z = dv.sig(V.tensor_copy, idx[:, slot, last:T], idx[:, 0, last:T])
                dv.wait(m, z)
                dv.sig(V.tensor_copy, idx[:, slot, t0:last], acc[:, 0, t0:last])
                settled[which, g] = dv.sig(V.tensor_copy, idx[0:LAST, slot, last:T], acc[0:LAST, 0, last:T])
            gp.wait(settled[which, g])

        def send(which, t):
            slot = VIEW[which][2]
            off = bass.IndirectOffsetOnAxis(ap=idx[:, slot, t:t + 1], axis=0)
            if which == "r":
                gp.dma(s_sr, G.indirect_dma_start, out=RKd, out_offset=off, in_=rec[:, t, :], in_offset=None)
            else:
                gp.dma(s_cr, G.indirect_dma_start, out=XWd, out_offset=off, in_=XWn[:, t, :], in_offset=None)

        def fetch(n=1):
            for _ in range(n):
                if fetched:
                    t = fetched.pop(0)
                    gp.dma(s_AT[t], G.indirect_dma_start, out=AT[:, t, :], out_offset=None, in_=ATd,
                           in_offset=bass.IndirectOffsetOnAxis(ap=idx[:, 3, t:t + 1], axis=0))

        fetched = list(range(T))
        dv.wait(view_ok["r"])
        dv.sig(V.tensor_copy, rec[:, :, 0].bitcast(U32), idx[:, 0, :])
        e = dv.sig(V.tensor_copy, rec[:, :, 1], srow)
        gp.wait(e)
        rank_start("r")
        g = 0
        for lt in range(T):
            rank_step("r", lt)
            t0, nt, _ = PARTS["r"][g]
            if g < 3 and lt == t0 + nt:
                settle("r", g)
                for t in range(t0, t0 + nt):
                    send("r", t)
                g += 1
        settle("r", 3)
        for t in range(18, T):
            send("r", t)
        gp.wait((s_sr, 16 * T))
        gp.dma(s_rt, G.dma_start, rec[:, :, :], RKd.rearrange("(t p) c -> p t c", p=P))
        perm_ok = (s_rt, 16)
        gp.wait(perm_ok, p2_end, (s_ATd, 32))
        e = gp.sig(G.tensor_copy, idx[:, 3, :], rec[:, :, 0].bitcast(U32))
        gp.wait(e)
        fetch(7)

        def references():
            nonlocal r_ok, ref_ok, rmax_ok, wl_ok, w_ok, wt_ok
            dv.wait(perm_ok, sel_ok)
            r_ok = dv.sig(V.tensor_copy, rsrt, rec[:, :, 1])
            copies = rs4[:, 0:126].rearrange("p (k c) -> p k c", k=3)
            m = dv.sig(V.tensor_copy, copies[:, :, 0:21], rec[:, 1:T, 1].unsqueeze(1).broadcast_to([P, 3, T - 1]))
            m = dv.sig(V.tensor_copy, copies[:, :, 21:42], rec[:, 0:T - 1, 1].unsqueeze(1).broadcast_to([P, 3, T - 1]))
            pe.wait(m, r_ok, *settled.values())
            m = pe.sig(TE.transpose, PSALL[:, 0, 0:P], rs4, ident[:, :])
            m2 = pe.sig(TE.matmul, PSALL[:, 1, 0:T], selr, rsrt, start=True, stop=True)
            dv.wait(m, m2)
            ref_ok = dv.sig(V.tensor_copy, ref, PSALL[:, 0, 0:1])
            rmax_ok = dv.sig(V.tensor_reduce, is0, PSALL[:, 0, 0:P], AX.X, ALU.max)
            wl_ok = r = dv.sig(V.tensor_tensor, wl, rsrt, PSALL[:, 1, 0:T], ALU.subtract)
            dv.wait(r)
            r = dv.sig(V.tensor_scalar, wu, wl, WMAX, None, ALU.min)
            ac_.wait(r)
            m = ac_.sig(S.activation, wu, wu, ACT.Exp)
            ac_.wait(m)
            w_ok = ac_.sig(S.activation, wl, wl, ACT.Exp, scale=SLOPE)
            e = w3_zero
            dv.wait(w_ok, e)
            for q in range(3):
                for src, start in ((wu[:, 1:T], P + 42 * q), (wl[:, 0:T - 1], 21 + 42 * q)):
                    cols = slice(start, start + (T - 2) * (P + 1) + 1, P + 1)
                    h = dv.sig(V.tensor_copy, W3[0][:, cols], src)
                    dv.wait(h)
                    wt_ok = dv.sig(V.tensor_tensor, W3[1][:, cols], src, W3[0][:, cols], ALU.subtract)

        def block_sums(t):
            pe.wait(wt_ok, w_ok, *settled.values(), *bfree.values())
            pe.wait((s_AT[t], 32))
            for c, (c0, w) in enumerate(CH):
                for q in range(2):
                    args = (PSALL[:, c, 0:w], W3[q][:, t * P:(t + 1) * P], AT[:, t, c0:c0 + w])
                    m = pe.sig(TE.matmul, *args, start=(t == 0 and q == 0), stop=(t == T - 1 and q == 1))
                sum_ok[c] = m
            return m

        sum_ok = {}
        tab_ok = {}
        r_ok = ref_ok = rmax_ok = wl_ok = w_ok = wt_ok = None
        dv.wait(view_ok["c"], xwn_ok)
        e = dv.sig(V.tensor_copy, XWn[:, :, D], scol)
        gp.wait(e)
        rank_start("c")
        summed = 0
        g = 0
        for lt in range(T):
            rank_step("c", lt)
            t0, nt, _ = PARTS["c"][g]
            if lt == REFS:
                references()
            if lt == min(t0 + nt, T - 1) and g < 2:
                settle("c", g)
                for t in range(t0, t0 + nt):
                    send("c", t)
                    if t % 2:
                        fetch()
                fetch(2)
                g += 1
            if lt > 7 and lt % 2:
                block_sums(summed)
                summed += 1
        settle("c", 2)
        for t in range(14, T):
            send("c", t)
        fetch(0)
        gp_xw = (s_cr, 16 * T)
        sp.wait(gp_xw)
        sp.dma(s_ct, nc.sync.dma_start, cs.unsqueeze(2), XWd[:, D:D + 1].rearrange("(t p) u -> p t u", p=P),
               allow_slow_non_contiguous=True)
        cs_ok = (s_ct, 16)
        gp.wait(cs_ok)
        fetch(T)

        for t in range(summed, MID):
            block_sums(t)

        dv.wait(cs_ok, *c_free[0], *c_free[1], *c_free[2])
        m = dv.sig(V.tensor_tensor, zt.rearrange("p (t j) -> p t j", t=T),
                   ident[:, :].unsqueeze(1).broadcast_to([P, T, P]), cs.unsqueeze(2).broadcast_to([P, T, P]), ALU.mult)
        pe.wait(m, sel_ok)
        bfree = {6: settled["c", 1], 7: settled["c", 2]}
        pe.wait(ref_ok)
        for g, (t0, nb) in enumerate(GRP):
            b = 6 + g % 2
            pe.wait(bfree[b])
            m = pe.sig(TE.matmul, PSALL[:, b, 0:nb * P], onesf, zt[:, t0 * P:(t0 + nb) * P], start=True, stop=True)
            dv.wait(m)
            bfree[b] = cb_ok = dv.sig(V.tensor_copy, cb[:, t0 * P:(t0 + nb) * P], PSALL[:, b, 0:nb * P])
        zt_free = m

        dv.wait(ref_ok, rmax_ok, cb_ok)
        cb3 = cb[:, :].rearrange("p (t j) -> p t j", t=T)
        low = mk2[:, 0:T]
        m = dv.sig(V.tensor_scalar, mk[:, :], cb3[:, :, 0], ref, 0.0, ALU.add, ALU.is_gt)
        dv.sig(V.tensor_scalar, low[:, 0:T - 1], cb3[:, 0:T - 1, P - 1], is0, 0.0, ALU.add, ALU.is_le)
        m2 = dv.sig(V.tensor_scalar, low[:, T - 1:T], cb3[:, T - 1:T, LAST - 1], is0, 0.0, ALU.add, ALU.is_le)
        dv.wait(m, m2, w_in)
        m = dv.sig(V.tensor_scalar, low, low, is_l, None, ALU.mult)
        dv.wait(m)
        m = dv.sig(V.scalar_tensor_tensor, mk[:, :], mk[:, :], is_u, low, ALU.mult, ALU.add)
        mk_ok = m
        for t in range(MID, MID + 3):
            block_sums(t)
        pe.wait(mk_ok, *bfree.values())
        m = pe.sig(TE.matmul, PSALL[0:1, 6, 0:T], n_below, mk[:, :], start=True, stop=True)
        m2 = pe.sig(TE.matmul, PSALL[0:1, 7, 0:T], n_above, mk[:, :], start=True, stop=True)
        win_mm = (m, m2)
        for t in range(MID + 3, T):
            w3_free = block_sums(t)

        sp.wait(w3_free)
        sp.dma(s_xw, nc.sync.dma_start, XWs, XWd[:, 0:D].rearrange("(t p) d -> p t d", p=P))
        XWs_ok = (s_xw, 16)
        den_ok = {}
        den_free = {}
        den_at = {}
        vreg, areg, preg = {}, {}, {}

        def window(e, reg):
            def load(jt):
                reg["lo"] = e.value_load(win[0:1, jt:jt + 1], min_val=0, max_val=T)
                reg["hi"] = e.value_load(win[0:1, T + jt:T + jt + 1], min_val=0, max_val=T)
            return load

        def place(e, reg):
            def load(jt):
                reg["base"] = e.value_load(win[0:1, 2 * T + jt:2 * T + jt + 1], min_val=0, max_val=T - WN)
                reg["wide"] = e.value_load(win[0:1, 3 * T + jt:3 * T + jt + 1], min_val=0, max_val=1)
            return load

        def width(e, reg):
            def load(jt):
                reg["wide"] = e.value_load(win[0:1, 3 * T + jt:3 * T + jt + 1], min_val=0, max_val=1)
            return load

        def den(jt, stage):
            s = jt % 2
            f3 = fw.rearrange("p (t j) -> p t j", t=WN)
            d3 = den_f[s].rearrange("p (t j) -> p t j", t=T)
            cbj = cb3[:, jt, :].unsqueeze(1)
            hi_, lo_ = den_b[s][:, :, 0, :], den_b[s][:, :, 1, :]

            def now(*a):
                return lambda: a

            def at(part):
                return lambda reg: part[:, bass.ds(reg["base"], WN), :]

            if stage == 0:
                dv.wait(win_ok)
                dv.do(place(V, vreg), jt)
                dv.wait(cb_ok, r_ok, gp_xw, *c_free[0], *c_free[1], *c_free[2], den_free.get(jt - 2), den_ok.get(jt - 1))
                if jt == 1:
                    dv.wait(E_ok)
                den_at[jt, 0] = dv.either(
                    lambda: vreg["wide"],
                    [(V.tensor_tensor, lambda: (f3, cbj.broadcast_to([P, WN, P]),
                                                rsrt[:, bass.ds(vreg["base"], WN)].unsqueeze(2).broadcast_to([P, WN, P]),
                                                ALU.add), {}),
                     (V.scalar_tensor_tensor, now(fw, fw, SLOPE, fw, ALU.mult, ALU.max), {})],
                    [(V.tensor_tensor, now(d3, cbj.broadcast_to([P, T, P]), rsrt.unsqueeze(2).broadcast_to([P, T, P]),
                                           ALU.add), {}),
                     (V.scalar_tensor_tensor, now(den_f[s], den_f[s], SLOPE, den_f[s], ALU.mult, ALU.max), {})])
            elif stage == 1:
                ac_.wait(win_ok)
                ac_.do(width(S, areg), jt)
                ac_.wait(den_at[jt, 0])
                den_at[jt, 1] = ac_.either(
                    lambda: areg["wide"],
                    [(S.activation, now(fw, fw, ACT.Exp), {})],
                    [(S.activation, now(den_f[s], den_f[s], ACT.Exp), {})])
            else:
                dv.wait(den_at[jt, 1])
                wide = []
                for t0, nb in GRP:
                    f = f3[:, 0:nb, :]
                    wide += [(V.tensor_copy, now(f, d3[:, t0:t0 + nb, :]), {}),
                             (V.tensor_copy, now(hi_[:, t0:t0 + nb, :], f), {}),
                             (V.tensor_tensor, now(lo_[:, t0:t0 + nb, :], f, hi_[:, t0:t0 + nb, :], ALU.subtract), {})]
                den_ok[jt] = dv.either(
                    lambda: vreg["wide"],
                    [(V.tensor_copy, lambda: (at(hi_)(vreg), f3), {}),
                     (V.tensor_tensor, lambda: (at(lo_)(vreg), f3, at(hi_)(vreg), ALU.subtract), {})],
                    wide)

        dv.wait(zt_free)
        m = dv.sig(V.tensor_scalar, zt, cb[:, :], ref, None, ALU.add)
        dv.wait(m)
        m = dv.sig(V.scalar_tensor_tensor, zt, zt, SLOPE, zt, ALU.mult, ALU.max)
        ac_.wait(m)
        e = ac_.sig(S.activation, zt, zt, ACT.Exp)
        dv.wait(*win_mm)
        lof, hif, bf, ff = (winf[0:1, q * T:(q + 1) * T] for q in range(4))
        a1 = dv.sig(V.tensor_copy, lof, PSALL[0:1, 6, 0:T])
        a2 = dv.sig(V.tensor_scalar, hif, PSALL[0:1, 7, 0:T], -1.0, float(T), ALU.mult, ALU.add)
        dv.wait(a1, a2)
        dv.sig(V.tensor_scalar, bf, lof, float(T - WN), None, ALU.min)
        a1 = dv.sig(V.tensor_tensor, ff, hif, lof, ALU.subtract)
        dv.wait(a1)
        a1 = dv.sig(V.tensor_scalar, ff, ff, WN + 0.5, None, ALU.is_gt)
        dv.wait(a1)
        win_ok = dv.sig(V.tensor_copy, win[0:1, :], winf[0:1, :])
        for stage in range(3):
            den(0, stage)
        dv.wait(e, (s_x1, 16), xw_end)
        m = dv.sig(V.tensor_tensor, zt.rearrange("p (t j) -> p t j", t=T), zt.rearrange("p (t j) -> p t j", t=T),
                   mk[:, :].unsqueeze(2).broadcast_to([P, T, P]), ALU.mult)
        ac_.wait(m, (s_x1, 16))
        h = ac_.sig(S.activation, Ehi, zt, ACT.Copy)
        dv.wait(h)
        E_ok = dv.sig(V.scalar_tensor_tensor, EX, Ehi, e_part, zt, ALU.mult, ALU.add)

        for c, (c0, w) in enumerate(CH):
            ac_.wait(sum_ok[c])
            h = ac_.sig(S.activation, tab[:, c0:c0 + w], PSALL[:, c, 0:w], ACT.Copy)
            dv.wait(h)
            tab_ok[c] = dv.sig(V.scalar_tensor_tensor, tab[:, c0:c0 + w], tab[:, c0:c0 + w], tab_part,
                            PSALL[:, c, 0:w], ALU.mult, ALU.add)

        def mixed(s, pair):
            with TE.If(preg["lo"] < preg["hi"]):
                with TE.Fori(preg["lo"], preg["hi"]) as k:
                    for part in range(2):
                        d = den_b[s][:, bass.ds(k, 1), part, :].rearrange("p o j -> p (o j)")
                        for b, c0, w in pair:
                            TE.matmul(PSALL[:, b, 0:w], d, AT[:, bass.ds(k, 1), c0:c0 + w].rearrange("p o j -> p (o j)"),
                                      start=False, stop=False)

        num_free = {6: win_ok, 7: win_ok}
        late_free = (w3_free, E_ok)
        z_free = [late_free] * NZ
        l_free = [E_ok] * NL
        steps = [(jt, c) for jt in range(T) for c in range(len(CH))]
        leaky_ok, sub_ok, exp_ok, g_ok, ln_ok = {}, {}, {}, {}, {}

        def tz(u):
            return tZ[u % NZ][:, 0:CH[steps[u][1]][1]]

        def tl(u):
            return tL[u % NL][:, 0:CH[steps[u][1]][1]]

        def num(v):
            jt = steps[2 * v][0]
            if v % 3 == 0:
                pe.wait(win_ok)
                pe.do(window(TE, preg), jt)
            pe.wait(den_ok[jt], num_free[6], num_free[7], E_ok, *(tab_ok[steps[2 * v + q][1]] for q in range(2)))
            pair = [(6 + q, *CH[steps[2 * v + q][1]]) for q in range(2)]
            for b, c0, w in pair:
                pe.do(TE.matmul, PSALL[:, b, 0:w], EX[:, jt * P:(jt + 1) * P], tab[:, c0:c0 + w],
                      start=True, stop=False)
            pe.do(mixed, jt % 2, pair)
            for q, (b, c0, w) in enumerate(pair):
                u = 2 * v + q
                m = pe.sig(TE.matmul, PSALL[:, b, 0:1], U[0:1, :], ones[0:1, :], start=False, stop=True)
                ac_.wait(m, l_free[u % NL], cst_ok)
                ln_ok[u] = num_free[b] = ac_.sig(S.activation, tl(u), PSALL[:, b, 0:w], ACT.Ln, bias=tiny)
            if v % 3 == 2:
                den_free[jt] = m

        def scores(u):
            jt, c = steps[u]
            c0, w = CH[c]
            ac_.wait(view_ok["r"], cs_ok, *z_free[u % NZ])
            z = ac_.sig(S.activation, tz(u), rb[:, c0:c0 + w], ACT.Identity, bias=cs[:, jt:jt + 1])
            dv.wait(z)
            leaky_ok[u] = dv.sig(V.scalar_tensor_tensor, tz(u), tz(u), SLOPE, tz(u), ALU.mult, ALU.max)

        def quotient(u):
            gp.wait(ln_ok[u], leaky_ok[u])
            sub_ok[u] = gp.sig(G.tensor_tensor, tz(u), tz(u), tl(u), ALU.subtract)

        def expo(u):
            ac_.wait(sub_ok[u])
            exp_ok[u] = ac_.sig(S.activation, tz(u), tz(u), ACT.Exp)

        def guard(u):
            dv.wait(exp_ok[u])
            l_free[u % NL] = g_ok[u] = dv.sig(V.scalar_tensor_tensor, tz(u), tl(u), LNZ, tz(u), ALU.is_gt, ALU.mult)

        def ymm(u):
            jt, c = steps[u]
            c0, w = CH[c]
            pe.wait(g_ok[u], XWs_ok)
            m = pe.sig(TE.matmul, PSALL[:, c, 0:w], XWs[:, jt, :], tz(u),
                        start=(jt == 0), stop=(jt == T - 1))
            z_free[u % NZ] = (m,)
            return m

        for q in range(2):
            scores(q)
        n_pairs = len(steps) // 2
        LAG = 2
        DEN_AT = {'0s': 0, '1s': 1, '1e': 2}

        def place_den(where):
            stage = DEN_AT.get(f"{cp}{where}")
            if v < n_pairs and jt + 1 < T and stage is not None:
                den(jt + 1, stage)

        for v in range(n_pairs + LAG):
            if v < n_pairs:
                jt, cp = steps[2 * v][0], v % 3
                num(v)
                place_den("s")
                quotient(2 * v)
                quotient(2 * v + 1)
            if v >= LAG:
                for q in range(2):
                    y_end = ymm(2 * (v - LAG) + q)
            if v + 1 < n_pairs:
                for q in range(2):
                    scores(2 * v + 2 + q)
            place_den("m")
            if v < n_pairs:
                for q in range(2):
                    expo(2 * v + q)
                    guard(2 * v + q)
            place_den("e")
        g_ok = g_ok[len(steps) - 1]

        YT = R1[:, 0:NP]
        Y3 = R1[:, NP:2 * NP].rearrange("p (t d) -> p t d", t=T)
        Ys = XWs
        xp = R1[:, 2 * NP:3 * NP].bitcast(FP16).rearrange("p (t c d) -> p t c d", t=T, c=2)
        gp.wait(y_end, g_ok)
        yz = gp.sig(G.memset, YT[:, N:NP], 0.0)
        for c, (c0, w) in enumerate(CH):
            ev = ac_ if c % 2 else dv
            ev.wait(y_end, g_ok)
            if c % 2:
                yt_a = ac_.sig(S.activation, YT[:, c0:c0 + w], PSALL[:, c, 0:w], ACT.Copy)
            else:
                yt_d = dv.sig(V.tensor_copy, YT[:, c0:c0 + w], PSALL[:, c, 0:w])
        row_ok = dv.sig(V.memset, ring[0:1, 5, 0:P], 1.0)
        dv.wait(yt_a, yt_d, yz, row_ok)
        pe.wait(yt_a, yt_d, yz)
        bfree = {0: yt_a, 1: yt_a}
        y3_ok = {}
        for g, (t0, nb) in enumerate(GRP):
            b = g % 2
            pe.wait(bfree[b])
            for q in range(nb):
                m = pe.sig(TE.transpose, PSALL[:, b, q * P:(q + 1) * P], YT[:, (t0 + q) * P:(t0 + q + 1) * P],
                           ident[:, :])
            src = PSALL[:, b, 0:nb * P].rearrange("p (b d) -> p b d", b=nb)
            ev = ac_ if g % 2 else dv
            ev.wait(m, yt_d, yt_a)
            if g % 2:
                bfree[b] = y3_a = ac_.sig(S.activation, Y3[:, t0:t0 + nb, :], src, ACT.Copy)
            else:
                bfree[b] = y3_d = dv.sig(V.tensor_copy, Y3[:, t0:t0 + nb, :], src)
            y3_ok[g] = (bfree[b],)
        m = dv.sig(V.tensor_reduce, up_y, YT, AX.X, ALU.min)
        m2 = dv.sig(V.tensor_reduce, down_y, YT, AX.X, ALU.max)
        dv.wait(m, m2)
        y_pm = dv.sig(V.scalar_tensor_tensor, pm, up_y, -1.0, down_y, ALU.mult, ALU.max)
        y_up = scale_of(y_pm, 2, ring[0:1, 5, 0:P], row_ok, 1.0, up_y, down_y)
        Yv = Yd.rearrange("(t p) d -> p t d", p=P)
        sp.wait(*y3_ok[2], *y3_ok[1])
        sp.dma(s_Yd, nc.sync.dma_start, Yv[:, 0:12, :], Y3[:, 0:12, :])
        sp.wait(y3_a, y3_d)
        sp.dma(s_Yd, nc.sync.dma_start, Yv[:, 12:T, :], Y3[:, 12:T, :])
        sp.wait((s_Yg[0], 96))
        sp.dma(s_x1b, nc.sync.dma_start, AO3, x1d.rearrange("(t p) d -> p t d", p=P))
        x1b_ok = (s_x1b, 16)
        gp.wait((s_Yd, 32), y_end)
        for k, (t0, nt) in enumerate(SL):
            for t in range(t0, t0 + nt):
                gp.dma(s_Yg[k], G.indirect_dma_start, out=Ys[:, t, :], out_offset=None, in_=Yd,
                       in_offset=bass.IndirectOffsetOnAxis(ap=idx[:, 3, t:t + 1], axis=0))
        xp_ok = split2(Ys, xp, up_y, [((s_Yg[k], 16 * nt), y_end, y_up) for k, (_, nt) in enumerate(SL)], SL)
        bank_free = [y_up] * 8
        outs = {}
        late = None

        def store(item):
            it, mrow, fin = item
            ok = fin()
            q = it % HB
            sp.wait(ok)
            sp.dma(s_out[q], nc.sync.dma_start, out[it * P:it * P + mrow, :], hb[0:mrow, q, :])
            outs[it] = (s_out[q], 16 * (it // HB + 1))

        first = {}
        pe.wait(y3_a, y3_d, y_up)
        for (t0, nt), ok in zip(SL, xp_ok):
            pe.wait(ok)
            for it in range(6):
                for jt in range(t0, t0 + nt):
                    m = pe.sig(TE.matmul, PSALL[:, it, 0:2 * D], AT[:, jt, it * P:(it + 1) * P],
                               xp[:, jt, :, :].rearrange("p c d -> p (c d)"), start=(jt == 0), stop=(jt == T - 1))
                first[it] = (m, P, PSALL[:, it, 0:2 * D].rearrange("p (c d) -> p d c", c=2))
        for it in range(T):
            m, mrow, view = first[it] if it < 6 else spread(it, xp_ok, it % 6, xp)
            hh = hb[0:mrow, it % HB, :]
            dv.wait(m, outs.get(it - HB), x1b_ok)
            r = dv.sig(V.tensor_reduce, hh, view, AX.X, ALU.add)
            bank_free[it % 6] = r
            dv.wait(r)
            r = dv.sig(V.scalar_tensor_tensor, hh, hh, down_y[0:mrow, :], AO3[0:mrow, it, :], ALU.mult, ALU.add)
            _, fin = norm(hh, mrow, it, hh, r)
            if late is not None:
                store(late)
            late = (it, mrow, fin)
        store(late)
        sp.wait(*outs.values())
        sp.wait(*AT_in)

        block = ctx.enter_context(nc.Block())

        @block.sync
        def _(eng):
            sp.emit(eng)

        @block.gpsimd
        def _(eng):
            gp.emit(eng)

        @block.scalar
        def _(eng):
            eng.add_instruction(mybir.InstLoadActFuncSet(act_func_set_id=LN_EXP_SET, engine=mybir.EngineType.Activation,
                                                         name=nc.get_next_instruction_name()))
            ac_.emit(eng)

        @block.vector
        def _(eng):
            dv.emit(eng)

        @block.tensor
        def _(eng):
            pe.emit(eng)


def kernel(x, adj, L0_gnn_t, L0_gnn_alpha, L0_gnn_beta, L1_gnn_W, L1_gnn_a):
    import numpy as np
    import concourse.bacc as bacc
    from concourse.bass_utils import run_bass_kernel_spmd as run

    nc = bacc.Bacc("TRN2", target_bir_lowering=False, num_devices=1)
    x, adj = np.asarray(x), np.asarray(adj)
    xr = np.zeros((NP, D), x.dtype)
    xr[:N] = x
    at = np.zeros((NP, N), adj.dtype)
    at[:N] = adj.T
    kinds, copies = np.arange(P) % 42 < 21, np.arange(P) // 42
    used = copies < 3
    rowk = np.stack([used & kinds, used & ~kinds, -1.0 * (copies == 1), -1.0 * (copies == 2),
                     (copies == 0) & kinds, (copies == 0) & ~kinds], axis=1).astype(np.float32)
    arrays = {
        "x": xr, "adjT": at,
        "alpha": np.asarray(L0_gnn_alpha).reshape(1, 1), "beta": np.asarray(L0_gnn_beta).reshape(1, 1),
        "W": np.ascontiguousarray(L1_gnn_W), "a": np.ascontiguousarray(np.asarray(L1_gnn_a).reshape(2, D).T),
        "rowk": rowk,
    }
    args = [nc.dram_tensor(f"in_{k}", v.shape, mybir.dt.from_np(v.dtype), kind="ExternalInput").ap()
            for k, v in arrays.items()]
    args.append(nc.dram_tensor("out_0", (N, D), F32, kind="ExternalOutput").ap())
    adj_resnorm2_kernel(nc, *args)
    r = run(nc, [{f"in_{k}": v for k, v in arrays.items()}], core_ids=[0])
    return r.results[0]["out_0"]
```
